# Optimizing a Trainium2 kernel written in Bass

```python
import numpy as np
import jax
import jax.numpy as jnp

def _softmax(x, axis=-1):
    return jax.nn.softmax(x, axis=axis)

def _gelu(x):
    return jax.nn.gelu(x, approximate=True)

def _silu(x):
    return jax.nn.silu(x)

def _sigmoid(x):
    return jax.nn.sigmoid(x)

def _layernorm(x, axis=-1, eps=1e-05):
    m = jnp.mean(x, axis=axis, keepdims=True)
    v = jnp.var(x, axis=axis, keepdims=True)
    return (x - m) / jnp.sqrt(v + eps)

def _scatter_add(tgt, idx, src, axis=0):
    return tgt.at[idx].add(src)

def _segment_sum(src, seg, n):
    return jax.ops.segment_sum(src, seg, n)
kernel_name = 'mk_dlrm_tower_d1_rec_r8_bd5c98'

def setup_inputs(seed: int=0):
    np.random.seed(seed)
    _w = jnp.asarray

    def _rec_inputs():
        import jax
        import jax.numpy as jnp
        _tk = jax.random.key(seed)
        dense_ctx = jax.random.normal(jax.random.fold_in(_tk, 190), (2048, 16), jnp.float32)
        ids = jnp.stack([jax.random.randint(jax.random.fold_in(_tk, 200 + f), (2048,), 0, v, jnp.int32) for f, v in enumerate([125000, 1250, 125000, 12500, 1250, 125000, 12500, 12500, 12500, 1000, 12500, 1250, 1000, 12500, 1250, 125000, 1000, 1000, 1250, 1250, 125000, 1250, 1250, 1000, 125000, 1250])], axis=1)
        tbl_0 = 0.05 * jax.random.normal(jax.random.fold_in(_tk, 500 + 0), (125000, 32), jnp.float32)
        tbl_1 = 0.05 * jax.random.normal(jax.random.fold_in(_tk, 500 + 1), (1250, 32), jnp.float32)
        tbl_2 = 0.05 * jax.random.normal(jax.random.fold_in(_tk, 500 + 2), (125000, 32), jnp.float32)
        tbl_3 = 0.05 * jax.random.normal(jax.random.fold_in(_tk, 500 + 3), (12500, 32), jnp.float32)
        tbl_4 = 0.05 * jax.random.normal(jax.random.fold_in(_tk, 500 + 4), (1250, 32), jnp.float32)
        tbl_5 = 0.05 * jax.random.normal(jax.random.fold_in(_tk, 500 + 5), (125000, 32), jnp.float32)
        tbl_6 = 0.05 * jax.random.normal(jax.random.fold_in(_tk, 500 + 6), (12500, 32), jnp.float32)
        tbl_7 = 0.05 * jax.random.normal(jax.random.fold_in(_tk, 500 + 7), (12500, 32), jnp.float32)
        tbl_8 = 0.05 * jax.random.normal(jax.random.fold_in(_tk, 500 + 8), (12500, 32), jnp.float32)
        tbl_9 = 0.05 * jax.random.normal(jax.random.fold_in(_tk, 500 + 9), (1000, 32), jnp.float32)
        tbl_10 = 0.05 * jax.random.normal(jax.random.fold_in(_tk, 500 + 10), (12500, 32), jnp.float32)
        tbl_11 = 0.05 * jax.random.normal(jax.random.fold_in(_tk, 500 + 11), (1250, 32), jnp.float32)
        tbl_12 = 0.05 * jax.random.normal(jax.random.fold_in(_tk, 500 + 12), (1000, 32), jnp.float32)
        tbl_13 = 0.05 * jax.random.normal(jax.random.fold_in(_tk, 500 + 13), (12500, 32), jnp.float32)
        tbl_14 = 0.05 * jax.random.normal(jax.random.fold_in(_tk, 500 + 14), (1250, 32), jnp.float32)
        tbl_15 = 0.05 * jax.random.normal(jax.random.fold_in(_tk, 500 + 15), (125000, 32), jnp.float32)
        tbl_16 = 0.05 * jax.random.normal(jax.random.fold_in(_tk, 500 + 16), (1000, 32), jnp.float32)
        tbl_17 = 0.05 * jax.random.normal(jax.random.fold_in(_tk, 500 + 17), (1000, 32), jnp.float32)
        tbl_18 = 0.05 * jax.random.normal(jax.random.fold_in(_tk, 500 + 18), (1250, 32), jnp.float32)
        tbl_19 = 0.05 * jax.random.normal(jax.random.fold_in(_tk, 500 + 19), (1250, 32), jnp.float32)
        tbl_20 = 0.05 * jax.random.normal(jax.random.fold_in(_tk, 500 + 20), (125000, 32), jnp.float32)
        tbl_21 = 0.05 * jax.random.normal(jax.random.fold_in(_tk, 500 + 21), (1250, 32), jnp.float32)
        tbl_22 = 0.05 * jax.random.normal(jax.random.fold_in(_tk, 500 + 22), (1250, 32), jnp.float32)
        tbl_23 = 0.05 * jax.random.normal(jax.random.fold_in(_tk, 500 + 23), (1000, 32), jnp.float32)
        tbl_24 = 0.05 * jax.random.normal(jax.random.fold_in(_tk, 500 + 24), (125000, 32), jnp.float32)
        tbl_25 = 0.05 * jax.random.normal(jax.random.fold_in(_tk, 500 + 25), (1250, 32), jnp.float32)
        _rk = jax.random.fold_in(_tk, 7)
        W_top1 = 0.0606339 * jax.random.normal(jax.random.fold_in(_tk, 801), (272, 512), jnp.float32)
        W_top2 = 0.0441942 * jax.random.normal(jax.random.fold_in(_tk, 802), (512, 256), jnp.float32)
        W_top3 = 0.0625 * jax.random.normal(jax.random.fold_in(_tk, 803), (256, 1), jnp.float32)
        b_top1 = jnp.zeros((512,), jnp.float32)
        b_top2 = jnp.zeros((256,), jnp.float32)
        return (dense_ctx, ids, tbl_0, tbl_1, tbl_2, tbl_3, tbl_4, tbl_5, tbl_6, tbl_7, tbl_8, tbl_9, tbl_10, tbl_11, tbl_12, tbl_13, tbl_14, tbl_15, tbl_16, tbl_17, tbl_18, tbl_19, tbl_20, tbl_21, tbl_22, tbl_23, tbl_24, tbl_25, W_top1, b_top1, W_top2, b_top2, W_top3)
    dense_ctx, ids, tbl_0, tbl_1, tbl_2, tbl_3, tbl_4, tbl_5, tbl_6, tbl_7, tbl_8, tbl_9, tbl_10, tbl_11, tbl_12, tbl_13, tbl_14, tbl_15, tbl_16, tbl_17, tbl_18, tbl_19, tbl_20, tbl_21, tbl_22, tbl_23, tbl_24, tbl_25, W_top1, b_top1, W_top2, b_top2, W_top3 = _rec_inputs()

    def _L0_rec_setup():
        import jax, jax.numpy as jnp
        import numpy as np
        M_FIELDS = 26
        H1 = 128
        H2 = 128
        BATCH = 256
        EMB_K = 32

        def _cin_layer(x_prev, x0, W, b):
            return jnp.einsum('bik,bjk,hij->bhk', x_prev, x0, W) + b[None, :, None]
        key = jax.random.key(seed)
        k0, k1, k2, k3, k4 = jax.random.split(key, 5)
        inputs = jax.random.normal(k0, (BATCH, M_FIELDS, EMB_K), dtype=jnp.float32)
        W1 = jax.random.normal(k1, (H1, M_FIELDS, M_FIELDS), dtype=jnp.float32) * 0.05
        b1 = jax.random.normal(k2, (H1,), dtype=jnp.float32) * 0.05
        W2 = jax.random.normal(k3, (H2, H1, M_FIELDS), dtype=jnp.float32) * 0.05
        b2 = jax.random.normal(k4, (H2,), dtype=jnp.float32) * 0.05
        return {'inputs': inputs, 'W1': W1, 'b1': b1, 'W2': W2, 'b2': b2}
    _L0_rec_all = _L0_rec_setup()
    _L0_rec_in = {k: v for k, v in _L0_rec_all.items() if k in ('W1', 'b1', 'W2', 'b2')}
    del _L0_rec_all
    return {'dense_ctx': dense_ctx, 'ids': ids, 'tbl_0': tbl_0, 'tbl_1': tbl_1, 'tbl_2': tbl_2, 'tbl_3': tbl_3, 'tbl_4': tbl_4, 'tbl_5': tbl_5, 'tbl_6': tbl_6, 'tbl_7': tbl_7, 'tbl_8': tbl_8, 'tbl_9': tbl_9, 'tbl_10': tbl_10, 'tbl_11': tbl_11, 'tbl_12': tbl_12, 'tbl_13': tbl_13, 'tbl_14': tbl_14, 'tbl_15': tbl_15, 'tbl_16': tbl_16, 'tbl_17': tbl_17, 'tbl_18': tbl_18, 'tbl_19': tbl_19, 'tbl_20': tbl_20, 'tbl_21': tbl_21, 'tbl_22': tbl_22, 'tbl_23': tbl_23, 'tbl_24': tbl_24, 'tbl_25': tbl_25, 'W_top1': W_top1, 'b_top1': b_top1, 'W_top2': W_top2, 'b_top2': b_top2, 'W_top3': W_top3, 'L0_rec_W1': _L0_rec_in['W1'], 'L0_rec_b1': _L0_rec_in['b1'], 'L0_rec_W2': _L0_rec_in['W2'], 'L0_rec_b2': _L0_rec_in['b2']}

def reference(dense_ctx, ids, tbl_0, tbl_1, tbl_2, tbl_3, tbl_4, tbl_5, tbl_6, tbl_7, tbl_8, tbl_9, tbl_10, tbl_11, tbl_12, tbl_13, tbl_14, tbl_15, tbl_16, tbl_17, tbl_18, tbl_19, tbl_20, tbl_21, tbl_22, tbl_23, tbl_24, tbl_25, W_top1, b_top1, W_top2, b_top2, W_top3, L0_rec_W1, L0_rec_b1, L0_rec_W2, L0_rec_b2):
    import jax
    import jax.numpy as jnp

    def _L0_rec_ref(inputs, W1, b1, W2, b2):
        import jax, jax.numpy as jnp
        import numpy as np
        M_FIELDS = 26
        H1 = 128
        H2 = 128
        BATCH = 256
        EMB_K = 32

        def _cin_layer(x_prev, x0, W, b):
            return jnp.einsum('bik,bjk,hij->bhk', x_prev, x0, W) + b[None, :, None]
        x1 = _cin_layer(inputs, inputs, W1, b1)
        x2 = _cin_layer(x1, inputs, W2, b2)
        res = jnp.concatenate([x1, x2], axis=1)
        return jnp.sum(res, axis=-1)
    e = jnp.stack([tbl_0[ids[:, 0]], tbl_1[ids[:, 1]], tbl_2[ids[:, 2]], tbl_3[ids[:, 3]], tbl_4[ids[:, 4]], tbl_5[ids[:, 5]], tbl_6[ids[:, 6]], tbl_7[ids[:, 7]], tbl_8[ids[:, 8]], tbl_9[ids[:, 9]], tbl_10[ids[:, 10]], tbl_11[ids[:, 11]], tbl_12[ids[:, 12]], tbl_13[ids[:, 13]], tbl_14[ids[:, 14]], tbl_15[ids[:, 15]], tbl_16[ids[:, 16]], tbl_17[ids[:, 17]], tbl_18[ids[:, 18]], tbl_19[ids[:, 19]], tbl_20[ids[:, 20]], tbl_21[ids[:, 21]], tbl_22[ids[:, 22]], tbl_23[ids[:, 23]], tbl_24[ids[:, 24]], tbl_25[ids[:, 25]]], axis=1)
    z = _L0_rec_ref(e, L0_rec_W1, L0_rec_b1, L0_rec_W2, L0_rec_b2)
    z = z.reshape(z.shape[0], -1)
    h = jnp.concatenate([z, dense_ctx], axis=1)
    h = jnp.maximum(h @ W_top1 + b_top1, 0.0)
    h = jnp.maximum(h @ W_top2 + b_top2, 0.0)
    y = h @ W_top3
    return y

_drawn_inputs = setup_inputs


def setup_inputs(seed=0):
    import zlib

    import numpy as np

    out = dict(_drawn_inputs(seed))
    spreads = {'b_top1': (0.0, 2.0), 'b_top2': (0.0, 0.8)}
    factors = {'tbl_0': 8.0,
     'tbl_1': 8.0,
     'tbl_2': 8.0,
     'tbl_3': 8.0,
     'tbl_4': 8.0,
     'tbl_5': 8.0,
     'tbl_6': 8.0,
     'tbl_7': 8.0,
     'tbl_8': 8.0,
     'tbl_9': 8.0,
     'tbl_10': 8.0,
     'tbl_11': 8.0,
     'tbl_12': 8.0,
     'tbl_13': 8.0,
     'tbl_14': 8.0,
     'tbl_15': 8.0,
     'tbl_16': 8.0,
     'tbl_17': 8.0,
     'tbl_18': 8.0,
     'tbl_19': 8.0,
     'tbl_20': 8.0,
     'tbl_21': 7.965,
     'tbl_22': 8.0,
     'tbl_23': 8.0,
     'tbl_24': 8.0,
     'tbl_25': 8.0,
     'L0_rec_W1': 7.993,
     'L0_rec_W2': 4.117,
     'dense_ctx': 5.896}
    for name, (base, spread) in spreads.items():
        noise = np.random.default_rng([zlib.crc32(name.encode()), seed]).standard_normal(out[name].shape)
        drawn = base * np.exp(spread * noise) if base else spread * noise
        out[name] = jnp.asarray(drawn.astype(out[name].dtype))
    for name, factor in factors.items():
        out[name] = (out[name] * factor).astype(out[name].dtype)
    return out
```

```python
import concourse.bass as bass
from concourse import mybir
from contextlib import ExitStack

F32 = mybir.dt.float32
ALU = mybir.AluOpType
ACT = mybir.ActivationFunctionType

P = 128
TOKENS, FIELDS, EMB, DENSE = 2048, 26, 32, 16
H1, H2, TOP1, TOP2 = 128, 128, 512, 256
TILES = TOKENS // P
TILES_PER_BLOCK = 4
BLOCKS = TILES // TILES_PER_BLOCK
BLOCK = TILES_PER_BLOCK * P
G = P // EMB
STEPS = P // G
HALF = STEPS // 2
BANK_STEPS = 4
BANKS_PER_HALF = HALF // BANK_STEPS
BANKS_PER_TILE = 2 * BANKS_PER_HALF

NA, NB_, NC = 9, 9, 8
A0, B0, C0 = 0, 9, 18
OFF_AB = [2 * sum(NA - x for x in range(d)) for d in range(NA)]
WITHIN_AB = NA * (NA + 1)
OFF_C = [WITHIN_AB + sum(NC - x for x in range(d)) for d in range(NC)]
WITHIN = WITHIN_AB + NC * (NC + 1) // 2
CROSS = NA * NB_
SECOND = CROSS + FIELDS
COLS = WITHIN + SECOND
ONE = FIELDS
FIELDS1 = FIELDS + 1
SECOND_FROM = 3
SECOND_FIELDS = FIELDS1 - SECOND_FROM
KEPT = NC + 1

ROW_B = NA * FIELDS
WID_B = FIELDS - B0
ROW_C = ROW_B + NB_ * WID_B
PAIRS = ROW_C + NC * NC
W = PAIRS + 1

ONE2, ONE1, FIRST1 = NC, NC + 1, NC + 2
SLOTS = NC + 2 + NC


def build(nc, dense_ctx, ids, tables, w_top1, b_top1, w_top2, b_top2, w_top3, w1, b1, w2, b2, out):
    ctx = ExitStack()
    with ctx:
        def sb(name, shape, dt=F32):
            return ctx.enter_context(nc.sbuf_tensor(name, shape, dt))

        def sem(name):
            return ctx.enter_context(nc.semaphore(name))

        ids_all = sb("ids_all", [P, TILES, FIELDS], mybir.dt.int32)
        ids_now = sb("ids_now", [P, TILES_PER_BLOCK, FIELDS], mybir.dt.int32)
        rows = [sb(f"rows{i}", [P, FIELDS * EMB]) for i in range(2)]
        raw = sb("raw", [P, STEPS, FIELDS])
        pairs = [sb(f"pairs{i}", [P, HALF, COLS]) for i in range(2)]
        diag = [sb(f"diag{i}", [P, HALF, FIELDS1, G]) for i in range(2)]
        trip1 = sb("trip1", [P, FIELDS1, BLOCK])
        trip2 = sb("trip2", [P, KEPT, BLOCK])
        weights1 = sb("weights1", [P, FIELDS1, P])
        weights2 = sb("weights2", [P, SLOTS, P])
        pair_w = sb("pair_w", [P, W])
        identity = sb("identity", [P, P])
        top1 = sb("top1", [P, 2, TOP1])
        top1_dense = sb("top1_dense", [DENSE, TOP1])
        top2 = sb("top2", [P, TOP1 // P, TOP2])
        top3 = sb("top3", [P, TOP2 // P])
        bias = sb("bias", [P, 2])
        bias_top1 = sb("bias_top1", [P, TOP1 // P])
        bias_top2 = sb("bias_top2", [P, TOP2 // P])
        dense_rows = sb("dense_rows", [P, TILES, DENSE])
        dense_t = sb("dense_t", [DENSE, TOKENS])
        y_all = sb("y_all", [1, TOKENS])
        late = sb("late", [P, 8 * BLOCK])
        z = late[:, 0:2 * BLOCK].rearrange("p (m n) -> p m n", n=BLOCK)
        hid1 = late[:, 2 * BLOCK:6 * BLOCK].rearrange("p (m n) -> p m n", n=BLOCK)
        hid2 = late[:, 6 * BLOCK:8 * BLOCK].rearrange("p (m n) -> p m n", n=BLOCK)
        wide1 = late[:, 0:FIELDS1 * WITHIN].rearrange("p (j c) -> p j c", c=WITHIN)
        wide2 = sb("wide2", [P, SLOTS, SECOND])
        w2_rows = trip2[:, :, :].rearrange("p j n -> p (j n)")[:, 0:H1 * FIELDS].rearrange(
            "p (i j) -> p i j", j=FIELDS)
        w2_t = weights1[:, 0:FIELDS, :]
        w1_rows = trip2[:, :, :].rearrange("p j n -> p (j n)")[:, H1 * FIELDS:H1 * FIELDS + FIELDS * FIELDS]
        sums_flat = trip1[:, :, :].rearrange("p j n -> p (j n)")[:, 0:FIELDS1 * W]
        sums = sums_flat.rearrange("p (j c) -> p j c", c=W)

        acc_first = [ctx.enter_context(nc.psum_tensor(f"acc_first{i}", [P, 512], F32)) for i in range(2)]
        acc_second = [ctx.enter_context(nc.psum_tensor(f"acc_second{i}", [P, 512], F32)) for i in range(2)]
        acc_z = [ctx.enter_context(nc.psum_tensor(f"acc_z{i}", [P, 512], F32)) for i in range(2)]
        acc_mlp = [ctx.enter_context(nc.psum_tensor(f"acc_mlp{i}", [P, 512], F32)) for i in range(2)]
        ring = acc_first + acc_second

        ids_loaded = sem("ids_loaded")
        ids_copied = sem("ids_copied")
        w1_loaded = sem("w1_loaded")
        w2_loaded = sem("w2_loaded")
        dense_loaded = sem("dense_loaded")
        small_loaded = sem("small_loaded")
        identity_ready = sem("identity_ready")
        identity_ones = sem("identity_ones")
        consts_ready = sem("consts_ready")
        pair_w_ready = sem("pair_w_ready")
        pair_w_raw = sem("pair_w_raw")
        ring_filled = sem("ring_filled")
        ring_emptied = sem("ring_emptied")
        wide_step = sem("wide_step")
        wide_ready = sem("wide_ready")
        gathered = [sem(f"gathered{i}") for i in range(2)]
        tiles_begun = sem("tiles_begun")
        rows_free = sem("rows_free")
        raw_ready = sem("raw_ready")
        half_ready = sem("half_ready")
        triples_done = sem("triples_done")
        triples_copied = sem("triples_copied")
        z_done = sem("z_done")
        z_copied = sem("z_copied")
        mlp_done = sem("mlp_done")
        mlp_copied = sem("mlp_copied")
        y_stored = sem("y_stored")

        w2_jobs = [range(j, min(j + 4, FIELDS)) for j in range(0, FIELDS, 4)]
        dense_jobs = [range(t, t + 4) for t in range(0, TILES, 4)]
        wide1_jobs = [range(j, min(j + 4, FIELDS1)) for j in range(0, FIELDS1, 4)]
        wide2_jobs = [range(j, min(j + 4, SLOTS)) for j in range(0, SLOTS, 4)]
        SUMS_FROM = len(w2_jobs)
        DENSE_FROM = SUMS_FROM + FIELDS
        WIDE1_FROM = DENSE_FROM + len(dense_jobs)
        WIDE2_FROM = WIDE1_FROM + len(wide1_jobs)
        JOBS = WIDE2_FROM + len(wide2_jobs)
        MLP_BANKS = TOP1 // P + TOP2 // P + 1

        HALF_STEPS = G + 1 + NA + NC + 1

        block = ctx.enter_context(nc.Block())

        @block.sync
        def _(sp):
            by_lane = ids.rearrange("(n t g) f -> g t n f", g=G, t=STEPS)
            for g in range(G):
                sp.dma_start(ids_all[EMB * g:EMB * (g + 1), :, :], by_lane[g]).then_inc(ids_loaded, 16)
            sp.dma_start(w2_rows, w2).then_inc(w2_loaded, 16)
            sp.dma_start(w1_rows, w1.rearrange("i l m -> i (l m)")).then_inc(w1_loaded, 16)
            sp.dma_start(pair_w[:, PAIRS:W], b1.rearrange("(p o) -> p o", o=1)).then_inc(w1_loaded, 16)
            sp.dma_start(dense_rows[:, :, :], dense_ctx.rearrange("(n p) d -> p n d", p=P)).then_inc(
                dense_loaded, 16)
            for dst, src in (
                (bias[:, 0:1], b1.rearrange("(p o) -> p o", o=1)),
                (bias[:, 1:2], b2.rearrange("(p o) -> p o", o=1)),
                (bias_top1[:, :], b_top1.rearrange("(m p) -> p m", p=P)),
                (bias_top2[:, :], b_top2.rearrange("(m p) -> p m", p=P)),
                (top3[:, :], w_top3.rearrange("(m p) o -> p (m o)", p=P)),
                (top1[:, :, :], w_top1[0:H1 + H2, :].rearrange("(m p) n -> p m n", p=P)),
                (top1_dense[:, :], w_top1[H1 + H2:H1 + H2 + DENSE, :]),
                (top2[:, :, :], w_top2.rearrange("(m p) n -> p m n", p=P)),
            ):
                sp.dma_start(dst, src, allow_slow_non_contiguous=True).then_inc(small_loaded, 16)
            sp.wait_ge(mlp_copied, MLP_BANKS * BLOCKS + 1)
            sp.dma_start(out.rearrange("n o -> o n"), y_all[:, :]).then_inc(y_stored, 16)
            sp.wait_ge(y_stored, 16)

        @block.gpsimd
        def _(pool):
            nc.gpsimd.memset(identity[:, :], 1.0).then_inc(identity_ones, 1)
            pool.wait_ge(identity_ones, 1)
            nc.gpsimd.affine_select(out=identity[:, :], in_=identity[:, :], compare_op=ALU.is_equal,
                                    fill=0.0, base=0, pattern=[[-1, P]],
                                    channel_multiplier=1).then_inc(identity_ready, 1)
            pool.wait_ge(ids_loaded, 16 * G)
            with pool.Fori(0, BLOCKS) as i:
                for q in range(TILES_PER_BLOCK):
                    pool.wait_ge(rows_free, i * TILES_PER_BLOCK + (q + 1))
                    nc.gpsimd.tensor_copy(ids_now[:, q, :], ids_all[:, i * TILES_PER_BLOCK + q, :]).then_inc(
                        ids_copied, 1)
                    pool.wait_ge(ids_copied, i * TILES_PER_BLOCK + (q + 1))
                    pool.sem_inc(tiles_begun, 1)
                    for f in range(FIELDS):
                        nc.gpsimd.indirect_dma_start(
                            out=rows[q % 2][:, EMB * f:EMB * (f + 1)], out_offset=None, in_=tables[f],
                            in_offset=bass.IndirectOffsetOnAxis(ids_now[:, q, f:f + 1], 0),
                        ).then_inc(gathered[q % 2], 16)

        @block.vector
        def _(dve):
            dve.sem_inc(rows_free, 2)
            dve.sem_inc(half_ready, 1)
            for h in range(2):
                nc.vector.memset(diag[h][:, :, :, :], 0.0).then_inc(consts_ready, 1)
            nc.vector.memset(wide2[:, :, :], 0.0).then_inc(consts_ready, 1)
            dve.wait_ge(consts_ready, 3)
            for h in range(2):
                for g in range(G):
                    nc.vector.memset(diag[h][EMB * g:EMB * (g + 1), :, ONE, g], 1.0).then_inc(consts_ready, 1)

            dve.wait_ge(w1_loaded, 32)
            lm = w1_rows.rearrange("p (l m) -> p l m", m=FIELDS)
            ml = w1_rows.rearrange("p (m l) -> p l m", l=FIELDS)
            for l0, n, wid, at in ((A0, NA, FIELDS, 0), (B0, NB_, WID_B, ROW_B), (C0, NC, NC, ROW_C)):
                m0 = FIELDS - wid
                nc.vector.tensor_tensor(
                    pair_w[:, at:at + n * wid].rearrange("p (l m) -> p l m", m=wid),
                    lm[:, l0:l0 + n, m0:FIELDS], ml[:, l0:l0 + n, m0:FIELDS], ALU.add).then_inc(pair_w_raw, 1)
            dve.wait_ge(pair_w_raw, 3)
            for l0, n, wid, at in ((A0, NA, FIELDS, 0), (B0, NB_, WID_B, ROW_B), (C0, NC, NC, ROW_C)):
                first = l0 * (FIELDS + 1)
                nc.vector.tensor_copy(pair_w[:, at:at + (wid + 1) * (n - 1) + 1:wid + 1],
                                      w1_rows[:, first:first + (FIELDS + 1) * (n - 1) + 1:FIELDS + 1]
                                      ).then_inc(pair_w_ready, 1)
            dve.wait_ge(pair_w_ready, 3)
            nc.vector.tensor_copy(sums[:, ONE, :], pair_w[:, :]).then_inc(wide_step, 1)
            steps = [1]

            def settle():
                dve.wait_ge(wide_step, steps[0])

            def step(ins):
                steps[0] += 1
                ins.then_inc(wide_step, 1)

            dve.wait_ge(ring_emptied, DENSE_FROM)
            settle()

            def strided(first, stride, n, lo, num, by):
                v = sums_flat[:, first:first + stride * n].rearrange("p (l x) -> p x l", x=stride)
                return v[:, lo:lo + by * (num - 1) + 1:by, :]

            groups = (
                (A0, NA, 0, FIELDS, [(B0, NB_ + NC, 0, FIELDS, B0, 1)]),
                (B0, NB_, ROW_B, WID_B, [(A0, NA, B0, 1, 0, FIELDS), (C0, NC, ROW_B, WID_B, NB_, 1)]),
                (C0, NC, ROW_C, NC, [(A0, NA, C0, 1, 0, FIELDS), (B0, NB_, ROW_B + NB_, 1, 0, WID_B)]),
            )
            for l0, n, row, wid, _others in groups:
                for d in range(n):
                    at = (OFF_AB[d] + (n - d) * (l0 == B0)) if l0 != C0 else OFF_C[d]
                    first = row + d
                    step(nc.vector.tensor_copy(
                        wide1[:, :, at:at + n - d],
                        sums[:, :, first:first + (wid + 1) * (n - d - 1) + 1:wid + 1]))
            settle()
            for second in (False, True):
                for l0, n, _row, _wid, others in groups:
                    for c0, num, base, per_l, lo, by in others:
                        for d in range(n - second):
                            e = d + second
                            at = (OFF_AB[e] + (n - e) * (l0 == B0)) if l0 != C0 else OFF_C[e]
                            first = (l0 * W + per_l * e if second else (l0 + e) * W) + base
                            dst = wide1[:, c0:c0 + num, at:at + n - e]
                            step(nc.vector.tensor_tensor(
                                dst, dst, strided(first, W + per_l, n - e, lo, num, by), ALU.add))
                settle()
            by_c = wide2[:, 0:NC, 0:CROSS].rearrange("p c (a b) -> p c a b", b=NB_)
            rows_a = sums[:, :, 0:ROW_B].rearrange("p j (l m) -> p j l m", m=FIELDS)
            rows_b = sums[:, :, ROW_B:ROW_C].rearrange("p j (l m) -> p j l m", m=WID_B)
            for c in range(NC):
                step(nc.vector.tensor_tensor(
                    by_c[:, c], rows_a[:, C0 + c, :, B0:C0],
                    rows_a[:, B0:C0, :, C0 + c].rearrange("p b a -> p a b"), ALU.add))
            step(nc.vector.tensor_copy(wide2[:, ONE2, CROSS:SECOND], sums[:, 0:FIELDS, PAIRS]))
            w_a = pair_w[:, 0:ROW_B].rearrange("p (l m) -> p l m", m=FIELDS)
            w_b = pair_w[:, ROW_B:ROW_C].rearrange("p (l m) -> p l m", m=WID_B)
            step(nc.vector.tensor_copy(wide2[:, ONE1, 0:CROSS].rearrange("p (a b) -> p a b", b=NB_),
                                       w_a[:, :, B0:C0]))
            step(nc.vector.tensor_copy(wide2[:, FIRST1:SLOTS, CROSS:CROSS + NA],
                                       w_a[:, :, C0:FIELDS].rearrange("p l c -> p c l")))
            step(nc.vector.tensor_copy(wide2[:, FIRST1:SLOTS, CROSS + NA:CROSS + NA + NB_],
                                       w_b[:, :, NB_:WID_B].rearrange("p l c -> p c l")))
            settle()
            for c in range(NC):
                step(nc.vector.tensor_tensor(
                    by_c[:, c], by_c[:, c], rows_b[:, 0:NA, :, NB_ + c], ALU.add))
            settle()
            dve.wait_ge(small_loaded, 16 * 8)
            nc.vector.tensor_scalar(bias[:, :], bias[:, :], float(EMB), None, ALU.mult).then_inc(wide_ready, 1)
            dve.wait_ge(consts_ready, 3 + 2 * G)

            with dve.Fori(0, BLOCKS) as i:
                for q in range(TILES_PER_BLOCK):
                    dve.wait_ge(gathered[q % 2], i * (16 * FIELDS * TILES_PER_BLOCK // 2)
                                + 16 * FIELDS * (q // 2 + 1))
                    dve.wait_ge(half_ready, i * (2 * TILES_PER_BLOCK * HALF_STEPS) + (2 * q * HALF_STEPS + 1))
                    nc.vector.transpose(raw[:, :, :].rearrange("p t f -> p f t"),
                                        rows[q % 2][:, :].rearrange("p (f t) -> p f t", t=EMB)
                                        ).then_inc(raw_ready, 1)
                    dve.wait_ge(raw_ready, i * TILES_PER_BLOCK + (q + 1))
                    dve.sem_inc(rows_free, 1)
                    for h in range(2):
                        x = raw[:, HALF * h:HALF * (h + 1), :]
                        ab = x[:, :, A0:C0].rearrange("p t (s l) -> p t s l", s=2)
                        dst = pairs[h]
                        dve.wait_ge(triples_done, i * (BANKS_PER_TILE * TILES_PER_BLOCK)
                                    + BANKS_PER_HALF * (2 * q + h + 1))
                        for g in range(G):
                            lanes = slice(EMB * g, EMB * (g + 1))
                            nc.vector.tensor_copy(diag[h][lanes, :, 0:FIELDS, g], x[lanes]).then_inc(half_ready, 1)
                        nc.vector.tensor_copy(dst[:, :, WITHIN + CROSS:COLS], x).then_inc(half_ready, 1)
                        for d in range(NA):
                            nc.vector.tensor_tensor(
                                dst[:, :, OFF_AB[d]:OFF_AB[d] + 2 * (NA - d)].rearrange("p t (s l) -> p t s l", s=2),
                                ab[:, :, :, 0:NA - d], ab[:, :, :, d:NA], ALU.mult).then_inc(half_ready, 1)
                        for d in range(NC):
                            nc.vector.tensor_tensor(
                                dst[:, :, OFF_C[d]:OFF_C[d] + NC - d],
                                x[:, :, C0:FIELDS - d], x[:, :, C0 + d:FIELDS], ALU.mult).then_inc(half_ready, 1)
                        nc.vector.tensor_tensor(
                            dst[:, :, WITHIN:WITHIN + CROSS].rearrange("p t (a b) -> p t a b", b=NB_),
                            x[:, :, A0:B0].unsqueeze(3).broadcast_to([P, HALF, NA, NB_]),
                            x[:, :, B0:C0].unsqueeze(2).broadcast_to([P, HALF, NA, NB_]),
                            ALU.mult).then_inc(half_ready, 1)

        @block.tensor
        def _(pe):
            pe.sem_inc(triples_done, 2 * BANKS_PER_HALF)
            pe.sem_inc(z_done, 1)
            pe.wait_ge(identity_ready, 1)

            def take_bank(n):
                if n >= len(ring):
                    pe.wait_ge(ring_emptied, n - len(ring) + 1)
                return ring[n % len(ring)]

            pe.wait_ge(w2_loaded, 16)
            for n, job in enumerate(w2_jobs):
                bank = take_bank(n)
                for x, j in enumerate(job):
                    ins = nc.tensor.transpose(bank[:, P * x:P * (x + 1)], w2_rows[:, :, j], identity[:, :])
                ins.then_inc(ring_filled, 1)
            pe.wait_ge(pair_w_ready, 3)
            for j in range(FIELDS):
                bank = take_bank(SUMS_FROM + j)
                pe.wait_ge(ring_emptied, j // 4 + 1)
                nc.tensor.matmul(bank[:, 0:W], w2_t[:, j, :], pair_w[:, :], start=True, stop=True).then_inc(
                    ring_filled, 1)
            pe.wait_ge(dense_loaded, 16)
            for n, job in enumerate(dense_jobs):
                bank = take_bank(DENSE_FROM + n)
                for x, t in enumerate(job):
                    ins = nc.tensor.transpose(bank[0:DENSE, P * x:P * (x + 1)], dense_rows[:, t, :], identity[:, :])
                ins.then_inc(ring_filled, 1)
            pe.wait_ge(wide_ready, 1)
            for n, job in enumerate(wide1_jobs):
                bank = take_bank(WIDE1_FROM + n)
                for x, j in enumerate(job):
                    ins = nc.tensor.transpose(bank[0:WITHIN, P * x:P * (x + 1)], wide1[:, j, :], identity[:, :])
                ins.then_inc(ring_filled, 1)
            for n, job in enumerate(wide2_jobs):
                bank = take_bank(WIDE2_FROM + n)
                for x, j in enumerate(job):
                    ins = nc.tensor.transpose(bank[0:SECOND, P * x:P * (x + 1)], wide2[:, j, :], identity[:, :])
                ins.then_inc(ring_filled, 1)
            pe.wait_ge(ring_emptied, JOBS)
            pe.wait_ge(small_loaded, 16 * 8)

            with pe.Fori(0, BLOCKS) as i:
                for q in range(TILES_PER_BLOCK):
                    for h in range(2):
                        pe.wait_ge(half_ready, i * (2 * TILES_PER_BLOCK * HALF_STEPS)
                                   + (HALF_STEPS * (2 * q + h + 1) + 1))
                        for s in range(BANKS_PER_HALF):
                            n = BANKS_PER_TILE * q + BANKS_PER_HALF * h + s
                            pe.wait_ge(triples_copied, i * (2 * BANKS_PER_TILE * TILES_PER_BLOCK) + 2 * (n + 1))
                            for x in range(BANK_STEPS):
                                t = BANK_STEPS * s + x
                                nc.tensor.matmul(
                                    acc_first[n % 2][0:WITHIN, FIELDS1 * G * x:FIELDS1 * G * (x + 1)],
                                    pairs[h][:, t, 0:WITHIN],
                                    diag[h][:, t, :, :].rearrange("p j g -> p (j g)"), start=True, stop=True)
                                ins = nc.tensor.matmul(
                                    acc_second[n % 2][0:SECOND, SECOND_FIELDS * G * x:SECOND_FIELDS * G * (x + 1)],
                                    pairs[h][:, t, WITHIN:COLS],
                                    diag[h][:, t, SECOND_FROM:FIELDS1, :].rearrange("p j g -> p (j g)"),
                                    start=True, stop=True)
                            ins.then_inc(triples_done, 1)
                pe.wait_ge(triples_copied, (i + 1) * (2 * BANKS_PER_TILE * TILES_PER_BLOCK) + 4)
                nc.tensor.matmul(acc_z[0][:, :], weights1[0:WITHIN, ONE, :], trip1[0:WITHIN, ONE, :],
                                 start=True, stop=False)
                nc.tensor.matmul(acc_z[0][:, :], weights2[0:SECOND, ONE1, :], trip2[0:SECOND, NC, :],
                                 start=False, stop=False)
                for c in range(NC):
                    ins = nc.tensor.matmul(acc_z[0][:, :], weights2[0:SECOND, FIRST1 + c, :],
                                           trip2[0:SECOND, c, :], start=False, stop=(c == NC - 1))
                ins.then_inc(z_done, 1)
                for j in range(FIELDS):
                    nc.tensor.matmul(acc_z[1][:, :], weights1[0:WITHIN, j, :], trip1[0:WITHIN, j, :],
                                     start=(j == 0), stop=False)
                for c in range(NC):
                    nc.tensor.matmul(acc_z[1][:, :], weights2[0:CROSS, c, :], trip2[0:CROSS, c, :],
                                     start=False, stop=False)
                nc.tensor.matmul(acc_z[1][:, :], weights2[0:SECOND, ONE2, :], trip2[0:SECOND, NC, :],
                                 start=False, stop=True).then_inc(z_done, 1)
                base = i * MLP_BANKS + 1
                pe.wait_ge(z_copied, i * 2 + 2)
                for m in range(TOP1 // P):
                    pe.wait_ge(mlp_copied, base + max(m - 1, 0))
                    cols = slice(P * m, P * (m + 1))
                    nc.tensor.matmul(acc_mlp[m % 2][:, :], top1[:, 0, cols], z[:, 0, :], start=True, stop=False)
                    nc.tensor.matmul(acc_mlp[m % 2][:, :], top1[:, 1, cols], z[:, 1, :], start=False, stop=False)
                    nc.tensor.matmul(acc_mlp[m % 2][:, :], top1_dense[:, cols],
                                     dense_t[:, bass.ds(i * BLOCK, BLOCK)],
                                     start=False, stop=True).then_inc(mlp_done, 1)
                for m in range(TOP2 // P):
                    pe.wait_ge(mlp_copied, base + TOP1 // P)
                    for k in range(TOP1 // P):
                        ins = nc.tensor.matmul(acc_mlp[m % 2][:, :], top2[:, k, P * m:P * (m + 1)], hid1[:, k, :],
                                               start=(k == 0), stop=(k == TOP1 // P - 1))
                    ins.then_inc(mlp_done, 1)
                pe.wait_ge(mlp_copied, base + (MLP_BANKS - 1))
                for k in range(TOP2 // P):
                    ins = nc.tensor.matmul(acc_mlp[0][0:1, :], top3[:, k:k + 1], hid2[:, k, :],
                                           start=(k == 0), stop=(k == TOP2 // P - 1))
                ins.then_inc(mlp_done, 1)
                pe.wait_ge(mlp_copied, base + MLP_BANKS)

        @block.scalar
        def _(act):
            act.sem_inc(triples_copied, 4)
            act.sem_inc(mlp_copied, 1)

            def filled(n):
                act.wait_ge(ring_filled, n + 1)
                return ring[n % len(ring)]

            for n, job in enumerate(w2_jobs):
                bank = filled(n)
                nc.scalar.copy(w2_t[:, job[0]:job[-1] + 1, :],
                               bank[:, 0:P * len(job)].rearrange("p (j h) -> p j h", h=P)).then_inc(ring_emptied, 1)
            for j in range(FIELDS):
                bank = filled(SUMS_FROM + j)
                nc.scalar.copy(sums[:, j, :], bank[:, 0:W]).then_inc(ring_emptied, 1)
            for n in range(len(dense_jobs)):
                bank = filled(DENSE_FROM + n)
                nc.scalar.copy(dense_t[:, BLOCK * n:BLOCK * (n + 1)], bank[0:DENSE, :]).then_inc(ring_emptied, 1)
            for n, job in enumerate(wide1_jobs):
                bank = filled(WIDE1_FROM + n)
                nc.scalar.copy(weights1[0:WITHIN, job[0]:job[-1] + 1, :],
                               bank[0:WITHIN, 0:P * len(job)].rearrange("p (j h) -> p j h", h=P)
                               ).then_inc(ring_emptied, 1)
            for n, job in enumerate(wide2_jobs):
                bank = filled(WIDE2_FROM + n)
                nc.scalar.copy(weights2[0:SECOND, job[0]:job[-1] + 1, :],
                               bank[0:SECOND, 0:P * len(job)].rearrange("p (j h) -> p j h", h=P)
                               ).then_inc(ring_emptied, 1)

            act.wait_ge(small_loaded, 16 * 8)
            with act.Fori(0, BLOCKS) as i:
                act.wait_ge(z_done, i * 2 + 1)
                for n in range(BANKS_PER_TILE * TILES_PER_BLOCK):
                    act.wait_ge(triples_done, i * (BANKS_PER_TILE * TILES_PER_BLOCK)
                                + (2 * BANKS_PER_HALF + n + 1))
                    tokens = slice(BANK_STEPS * G * n, BANK_STEPS * G * (n + 1))
                    nc.scalar.copy(
                        trip1[0:WITHIN, :, tokens].rearrange("p j (t g) -> p t j g", g=G),
                        acc_first[n % 2][0:WITHIN, 0:BANK_STEPS * FIELDS1 * G].rearrange(
                            "p (t j g) -> p t j g", j=FIELDS1, g=G)).then_inc(triples_copied, 1)
                    nc.scalar.copy(
                        trip2[0:SECOND, :, tokens].rearrange("p j (t g) -> p t j g", g=G),
                        acc_second[n % 2][0:SECOND, 0:BANK_STEPS * SECOND_FIELDS * G].rearrange(
                            "p (t j g) -> p t j g", j=SECOND_FIELDS, g=G)[:, :, SECOND_FIELDS - KEPT:SECOND_FIELDS, :]
                    ).then_inc(triples_copied, 1)
                for m in range(2):
                    act.wait_ge(z_done, i * 2 + (m + 2))
                    nc.scalar.activation(z[:, m, :], acc_z[m][:, :], ACT.Identity,
                                         bias=bias[:, m:m + 1]).then_inc(z_copied, 1)
                for m in range(MLP_BANKS):
                    act.wait_ge(mlp_done, i * MLP_BANKS + (m + 1))
                    if m < TOP1 // P:
                        ins = nc.scalar.activation(hid1[:, m, :], acc_mlp[m % 2][:, :], ACT.Relu,
                                                   bias=bias_top1[:, m:m + 1])
                    elif m < MLP_BANKS - 1:
                        k = m - TOP1 // P
                        ins = nc.scalar.activation(hid2[:, k, :], acc_mlp[k % 2][:, :], ACT.Relu,
                                                   bias=bias_top2[:, k:k + 1])
                    else:
                        ins = nc.scalar.copy(y_all[:, bass.ds(i * BLOCK, BLOCK)], acc_mlp[0][0:1, :])
                    ins.then_inc(mlp_copied, 1)


_INS = (["dense_ctx", "ids"] + [f"tbl_{f}" for f in range(FIELDS)]
        + ["W_top1", "b_top1", "W_top2", "b_top2", "W_top3", "L0_rec_W1", "L0_rec_b1", "L0_rec_W2", "L0_rec_b2"])


def kernel(**inputs):
    import numpy as _np
    import concourse.bacc as _bacc
    from concourse import mybir as _mybir
    from concourse.bass_utils import run_bass_kernel_spmd as _run

    nc = _bacc.Bacc("TRN2", target_bir_lowering=False, num_devices=1)
    arrays, args = {}, []
    for name in _INS:
        a = _np.ascontiguousarray(inputs[name])
        arrays[f"in_{name}"] = a
        args.append(nc.dram_tensor(f"in_{name}", a.shape, _mybir.dt.from_np(a.dtype), kind="ExternalInput").ap())
    y = nc.dram_tensor("out_y", (TOKENS, 1), _mybir.dt.float32, kind="ExternalOutput").ap()
    build(nc, args[0], args[1], args[2:2 + FIELDS], *args[2 + FIELDS:], y)
    r = _run(nc, [arrays], core_ids=[0])
    return r.results[0]["out_y"]
```

```python
import concourse.bass as bass
from concourse import mybir
from contextlib import ExitStack

F32 = mybir.dt.float32
ALU = mybir.AluOpType
ACT = mybir.ActivationFunctionType

F16 = mybir.dt.float16
BF16 = mybir.dt.bfloat16

P = 128
TOKENS, FIELDS, EMB, DENSE = 2048, 26, 32, 16
H1, H2, TOP1, TOP2 = 128, 128, 512, 256
TILES = TOKENS // P
TILES_PER_BLOCK = 2
BLOCKS = TILES // TILES_PER_BLOCK
BLOCK = TILES_PER_BLOCK * P
G = P // EMB
STEPS = P // G
HALF = STEPS // 2
HALVES = 2 * TILES_PER_BLOCK
BANK_STEPS = 4
BANKS_PER_HALF = HALF // BANK_STEPS
BANKS_PER_TILE = 2 * BANKS_PER_HALF
BANKS_PER_BLOCK = TILES_PER_BLOCK * BANKS_PER_TILE

SMALL_FIELDS = (17,)
SMALL_ROWS = 1000
NSMALL = len(SMALL_FIELDS)
PER_PART = 8
SMALL_PARTS = SMALL_ROWS // PER_PART
SPLITS = 3
FIRST_SMALL = TILES_PER_BLOCK
SMALL_TILES = TILES - FIRST_SMALL

NA, NB_, NC = 9, 9, 8
A0, B0, C0 = 0, 9, 18
OFF_AB = [2 * sum(NA - x for x in range(d)) for d in range(NA)]
WITHIN_AB = NA * (NA + 1)
OFF_C = [WITHIN_AB + sum(NC - x for x in range(d)) for d in range(NC)]
WITHIN = WITHIN_AB + NC * (NC + 1) // 2
CROSS = NA * NB_
MIXED = NA + NB_
RAW_AB = CROSS + 1
SECOND = RAW_AB + MIXED
COLS = WITHIN + SECOND
ONE = FIELDS
FIELDS1 = FIELDS + 1
SECOND_FROM = 3
SECOND_FIELDS = FIELDS1 - SECOND_FROM
KEPT = NC + 1

ROW_B = NA * FIELDS
WID_B = FIELDS - B0
ROW_C = ROW_B + NB_ * WID_B
PAIRS = ROW_C + NC * NC
W = PAIRS + 1

GRAM_FIELDS = NC - 1
GRAM = GRAM_FIELDS * MIXED
ALL2 = SECOND + MIXED

ONE2, ONE1, SLOT_GRAM = NC, NC + 1, NC + 2
SLOTS = NC + 3

DENSE_PAIRS = [(a, b) for a in range(SPLITS) for b in range(SPLITS) if a + b < 2 * SPLITS - 2]
STACK = len(DENSE_PAIRS)


def build(nc, dense_ctx, ids, tables, w_top1, b_top1, w_top2, b_top2, w_top3, w1, b1, w2, b2, out):
    ctx = ExitStack()
    with ctx:
        def sb(name, shape, dt=F32):
            return ctx.enter_context(nc.sbuf_tensor(name, shape, dt))

        def sem(name):
            return ctx.enter_context(nc.semaphore(name))

        ids_all = sb("ids_all", [P, TILES + TILES_PER_BLOCK, FIELDS], mybir.dt.int32)
        ids_now = sb("ids_now", [P, TILES_PER_BLOCK, FIELDS], mybir.dt.int32)
        rows = [sb(f"rows{i}", [P, FIELDS * EMB]) for i in range(2)]
        raw = sb("raw", [P, STEPS, FIELDS])
        sums_flat = sb("sums", [P, FIELDS1 * W])
        sums = sums_flat[:, :].rearrange("p (j c) -> p j c", c=W)
        pairs = [sb(f"pairs{i}", [P, HALF, COLS])[:, :, :] for i in range(2)]
        diag = [sb(f"diag{i}", [P, HALF, FIELDS1, G])[:, :, :, :] for i in range(2)]
        at = 0
        for i in range(2):
            pairs.append(sums_flat[:, at:at + HALF * COLS].rearrange("p (t c) -> p t c", c=COLS))
            at += HALF * COLS
            diag.append(sums_flat[:, at:at + HALF * FIELDS1 * G].rearrange(
                "p (t j g) -> p t j g", j=FIELDS1, g=G))
            at += HALF * FIELDS1 * G
        top_parts = sums_flat[0:DENSE, at:at + SPLITS * TOP1 // 2].bitcast(BF16).rearrange(
            "p (s n) -> p s n", n=TOP1)
        trip1 = sb("trip1", [P, FIELDS1, BLOCK])
        trip2 = sb("trip2", [P, KEPT, BLOCK])
        weights1 = sb("weights1", [P, FIELDS1, P])
        gram = sb("gram", [P, BLOCK])
        weights2 = sb("weights2", [P, SLOTS, P])
        pair_w = sb("pair_w", [P, W])
        w1_rows = sb("w1_rows", [P, FIELDS * FIELDS])
        identity = sb("identity", [P, P])
        top1 = sb("top1", [P, 2, TOP1])
        top1_dense = sb("top1_dense", [DENSE, TOP1])
        top2 = sb("top2", [P, TOP1 // P, TOP2])
        top3 = sb("top3", [P, TOP2 // P])
        bias = sb("bias", [P, 2])
        bias_top1 = sb("bias_top1", [P, TOP1 // P])
        bias_top2 = sb("bias_top2", [P, TOP2 // P])
        dense_rows = sb("dense_rows", [P, TILES, DENSE])
        late = sb("late", [P, max(FIELDS1 * WITHIN, 8 * BLOCK)])
        z = late[:, 0:2 * BLOCK].rearrange("p (m n) -> p m n", n=BLOCK)
        hid1 = late[:, 2 * BLOCK:6 * BLOCK].rearrange("p (m n) -> p m n", n=BLOCK)
        hid2 = late[:, 6 * BLOCK:8 * BLOCK].rearrange("p (m n) -> p m n", n=BLOCK)
        wide1 = late[:, 0:FIELDS1 * WITHIN].rearrange("p (j c) -> p j c", c=WITHIN)
        wide2 = sb("wide2", [P, SLOTS, GRAM])
        w2_rows = pairs[1].rearrange("p t c -> p (t c)")[:, 0:H1 * FIELDS].rearrange(
            "p (i j) -> p i j", j=FIELDS)
        w2_t = weights1[:, 0:FIELDS, :]
        dense_all = sb("dense_all", [P, TOKENS])
        dense_t = dense_all[:, 0:TOKENS // 2].bitcast(BF16)
        dense_parts = dense_all[:, TOKENS // 2:TOKENS].bitcast(BF16).rearrange(
            "p (t s d) -> p t s d", s=STACK, d=DENSE)
        dense_w = sb("dense_w", [P, TOP1], BF16)
        identity_b = sb("identity_b", [P, P], BF16)
        y_now = sb("y_now", [1, BLOCK])
        found = sb("found", [P, SMALL_TILES, NSMALL * EMB])
        identity16 = sb("identity16", [P, P], F16)
        ids16 = sb("ids16", [P, TILES, NSMALL], F16)
        row_int = sb("row_int", [P, PER_PART], mybir.dt.int32)
        row_of = sb("row_of", [P, PER_PART])
        early = late[0:SMALL_PARTS, :]
        at = 0
        small_rows = early[:, at:at + NSMALL * PER_PART * EMB]
        at += NSMALL * PER_PART * EMB
        small_parts = early[:, at:at + NSMALL * PER_PART * SPLITS * EMB // 2].bitcast(BF16).rearrange(
            "p (f a s k) -> p f a s k", f=NSMALL, a=PER_PART, s=SPLITS)
        at += NSMALL * PER_PART * SPLITS * EMB // 2
        onehot = []
        for i in range(2):
            onehot.append(early[:, at:at + PER_PART * NSMALL * P // 2].bitcast(BF16).rearrange(
                "p (a f n) -> p a f n", f=NSMALL, n=P))
            at += PER_PART * NSMALL * P // 2
        ids_wide = dense_all[0:SMALL_PARTS, 0:SMALL_TILES * NSMALL * P // 2].bitcast(F16).rearrange(
            "p (t n) -> p t n", n=NSMALL * P)

        acc_first = [ctx.enter_context(nc.psum_tensor(f"acc_first{i}", [P, 512], F32)) for i in range(2)]
        acc_second = [ctx.enter_context(nc.psum_tensor(f"acc_second{i}", [P, 512], F32)) for i in range(2)]
        acc_z = [ctx.enter_context(nc.psum_tensor(f"acc_z{i}", [P, 512], F32)) for i in range(2)]
        acc_mlp = [ctx.enter_context(nc.psum_tensor(f"acc_mlp{i}", [P, 512], F32)) for i in range(2)]
        ring = acc_z + acc_mlp

        ids_loaded = sem("ids_loaded")
        ids_copied = sem("ids_copied")
        ids_padded = sem("ids_padded")
        first_ids = sem("first_ids")
        w1_loaded = sem("w1_loaded")
        w2_loaded = sem("w2_loaded")
        dense_loaded = sem("dense_loaded")
        small_loaded = sem("small_loaded")
        identity_ready = sem("identity_ready")
        identity_ones = sem("identity_ones")
        identity_b_ready = sem("identity_b_ready")
        consts_ready = sem("consts_ready")
        pair_w_ready = sem("pair_w_ready")
        pair_w_raw = sem("pair_w_raw")
        ring_filled = sem("ring_filled")
        ring_emptied = sem("ring_emptied")
        wide_step = sem("wide_step")
        wide_ready = sem("wide_ready")
        wide_own = sem("wide_own")
        ones_ready = sem("ones_ready")
        dense_split = sem("dense_split")
        top_split = sem("top_split")
        dense_w_loaded = sem("dense_w_loaded")
        gathered = [sem(f"gathered{i}") for i in range(2)]
        tiles_begun = sem("tiles_begun")
        rows_free = sem("rows_free")
        raw_ready = sem("raw_ready")
        half_ready = sem("half_ready")
        triples_done = sem("triples_done")
        triples_copied = sem("triples_copied")
        row_int_ready = sem("row_int_ready")
        small_consts = sem("small_consts")
        small_rows_loaded = sem("small_rows_loaded")
        small_split = sem("small_split")
        onehot_ready = sem("onehot_ready")
        small_done = sem("small_done")
        small_copied = sem("small_copied")
        found_copied = sem("found_copied")
        gram_ready = sem("gram_ready")
        z_done = sem("z_done")
        z_copied = sem("z_copied")
        mlp_done = sem("mlp_done")
        mlp_copied = sem("mlp_copied")
        y_stored = sem("y_stored")

        w2_jobs = [range(j, min(j + 4, FIELDS)) for j in range(0, FIELDS, 4)]
        dense_jobs = [range(t, t + 4) for t in range(0, TILES, 4)]
        wide1_jobs = [range(j, min(j + 4, FIELDS1)) for j in range(0, FIELDS1, 4)]
        wide2_jobs = [range(j, min(j + 4, SLOTS)) for j in range(0, SLOTS, 4)]
        per_bank = 512 // (NSMALL * P)
        ids_jobs = [range(t, min(t + per_bank, SMALL_TILES)) for t in range(0, SMALL_TILES, per_bank)]
        W2_FROM = len(ids_jobs)
        SUMS_FROM = W2_FROM + len(w2_jobs)
        WIDE1_FROM = SUMS_FROM + FIELDS
        WIDE2_FROM = WIDE1_FROM + len(wide1_jobs)
        DENSE_FROM = WIDE2_FROM + len(wide2_jobs)
        JOBS = DENSE_FROM + len(dense_jobs)
        MLP_AFTER = {0: 0, 1: 1, 2: 2, 3: 3, 5: 4, BANKS_PER_TILE - 1: 5}
        assert NA == BANKS_PER_TILE + 1
        LOOK_UP_FROM = 3
        RES1, RES2 = TOP1 // P, TOP2 // P
        RESULTS = RES1 + RES2 + 1
        OWN_COPIES = 2 * (NA + NB_ + NC)

        HALF_STEPS = G + 1 + NA + NC + 1

        def pair_column(l0, d):
            return OFF_C[d] if l0 == C0 else OFF_AB[d] + (NB_ - d) * (l0 == B0)

        def pair_run(c0, num, row, wid, n, d):
            return sums[:, c0:c0 + num, row + d:row + d + (wid + 1) * (n - d - 1) + 1:wid + 1]

        def through(i, q, each, more=0):
            return i * (TILES_PER_BLOCK * each) + (q * each + more)

        def columns(q):
            q %= TILES_PER_BLOCK
            return slice(P * q, P * (q + 1))

        def wait_for(eng, semaphore, value):
            if not isinstance(value, int) or value > 0:
                eng.wait_ge(semaphore, value)

        block = ctx.enter_context(nc.Block())

        @block.sync
        def _(sp):
            by_lane = ids.rearrange("(n t g) f -> g t n f", g=G, t=STEPS)
            for g in range(G):
                sp.dma_start(ids_all[EMB * g:EMB * (g + 1), 0:TILES, :], by_lane[g]).then_inc(ids_loaded, 16)
            for n, f in enumerate(SMALL_FIELDS):
                sp.dma_start(small_rows[:, PER_PART * EMB * n:PER_PART * EMB * (n + 1)],
                             tables[f].rearrange("(p a) k -> p (a k)", a=PER_PART)).then_inc(small_rows_loaded, 16)
            sp.dma_start(w2_rows, w2).then_inc(w2_loaded, 16)
            sp.dma_start(w1_rows[:, :], w1.rearrange("i l m -> i (l m)")).then_inc(w1_loaded, 16)
            sp.dma_start(pair_w[:, PAIRS:W], b1.rearrange("(p o) -> p o", o=1)).then_inc(w1_loaded, 16)
            sp.dma_start(dense_rows[:, :, :], dense_ctx.rearrange("(n p) d -> p n d", p=P)).then_inc(
                dense_loaded, 16)
            for dst, src in (
                (bias[:, 0:1], b1.rearrange("(p o) -> p o", o=1)),
                (bias[:, 1:2], b2.rearrange("(p o) -> p o", o=1)),
                (bias_top1[:, :], b_top1.rearrange("(m p) -> p m", p=P)),
                (bias_top2[:, :], b_top2.rearrange("(m p) -> p m", p=P)),
                (top3[:, :], w_top3.rearrange("(m p) o -> p (m o)", p=P)),
                (top1[:, :, :], w_top1[0:H1 + H2, :].rearrange("(m p) n -> p m n", p=P)),
                (top1_dense[:, :], w_top1[H1 + H2:H1 + H2 + DENSE, :]),
                (top2[:, :, :], w_top2.rearrange("(m p) n -> p m n", p=P)),
            ):
                sp.dma_start(dst, src, allow_slow_non_contiguous=True).then_inc(small_loaded, 16)
            def store_y(t):
                sp.wait_ge(mlp_copied, (t + 1) * RESULTS)
                sp.dma_start(out.rearrange("n o -> o n")[:, P * t:P * (t + 1)],
                             y_now[:, columns(t)]).then_inc(y_stored, 16)

            for t in range(TILES):
                cols = columns(t)
                sp.wait_ge(triples_copied, 2 * BANKS_PER_TILE * (t + 1))
                for c in range(GRAM_FIELDS):
                    sp.dma_start(gram[MIXED * c:MIXED * (c + 1), cols],
                                 trip2[RAW_AB:RAW_AB + MIXED, c, cols]).then_inc(gram_ready, 16)
                sp.dma_start(trip2[SECOND:ALL2, NC, cols],
                             trip2[RAW_AB:RAW_AB + MIXED, NC - 1, cols]).then_inc(gram_ready, 16)
                if t == 0:
                    sp.wait_ge(top_split, 2 * SPLITS - 1)
                    for n, (_a, b) in enumerate(DENSE_PAIRS):
                        sp.dma_start(dense_w[DENSE * n:DENSE * (n + 1), :], top_parts[:, b, :]).then_inc(dense_w_loaded, 16)
                else:
                    store_y(t - 1)
            store_y(TILES - 1)
            sp.wait_ge(y_stored, 16 * TILES)

        @block.gpsimd
        def _(pool):
            nc.gpsimd.memset(identity[:, :], 1.0).then_inc(identity_ones, 1)
            pool.wait_ge(identity_ones, 1)
            nc.gpsimd.affine_select(out=identity[:, :], in_=identity[:, :], compare_op=ALU.is_equal,
                                    fill=0.0, base=0, pattern=[[-1, P]],
                                    channel_multiplier=1).then_inc(identity_ready, 1)
            nc.gpsimd.iota(row_int[:, :], pattern=[[1, PER_PART]], base=0,
                           channel_multiplier=PER_PART).then_inc(row_int_ready, 1)
            pool.wait_ge(ids_loaded, 16 * G)

            def gather_block(i, fields):
                for q in range(TILES_PER_BLOCK):
                    wait_for(pool, rows_free, through(i, q, 1, -1))
                    if isinstance(i, int):
                        pool.wait_ge(first_ids, q + 1)
                    else:
                        pool.wait_ge(ids_copied, through(i, q, 1, -1))
                    pool.sem_inc(tiles_begun, 1)
                    for f in fields:
                        nc.gpsimd.indirect_dma_start(
                            out=rows[q % 2][:, EMB * f:EMB * (f + 1)], out_offset=None, in_=tables[f],
                            in_offset=bass.IndirectOffsetOnAxis(ids_now[:, q, f:f + 1], 0),
                        ).then_inc(gathered[q % 2], 16)

            for q in range(TILES_PER_BLOCK):
                nc.gpsimd.tensor_copy(ids_now[:, q, :], ids_all[:, q, :]).then_inc(first_ids, 1)
            gather_block(0, range(FIELDS))
            with pool.Fori(1, BLOCKS) as i:
                gather_block(i, [f for f in range(FIELDS) if f not in SMALL_FIELDS])

        @block.vector
        def _(dve):
            def set_diag(n):
                for h in (n, n + 1):
                    nc.vector.memset(diag[h].rearrange("p t j g -> p (t j g)").bitcast(BF16), 0.0).then_inc(consts_ready, 1)
                dve.wait_ge(consts_ready, 1 + n * (1 + G) + 2)
                for h in (n, n + 1):
                    for g in range(G):
                        nc.vector.memset(diag[h][EMB * g:EMB * (g + 1), :, ONE, g], 1.0).then_inc(consts_ready, 1)
                dve.wait_ge(consts_ready, 1 + (n + 2) * (1 + G))

            def set_ones(n):
                for h in (n, n + 1):
                    nc.vector.memset(pairs[h][:, :, WITHIN + CROSS:WITHIN + RAW_AB], 1.0).then_inc(ones_ready, 1)
                dve.wait_ge(ones_ready, n + 2)

            dve.wait_ge(row_int_ready, 1)
            nc.vector.tensor_copy(row_of[:, :], row_int[:, :]).then_inc(small_consts, 1)
            dve.wait_ge(identity_ready, 1)
            nc.vector.tensor_copy(identity16[:, :], identity[:, :]).then_inc(small_consts, 1)
            nc.vector.tensor_copy(identity_b[:, :], identity[:, :]).then_inc(identity_b_ready, 1)
            nc.vector.memset(ids_all[:, TILES:TILES + TILES_PER_BLOCK, :], 0).then_inc(ids_padded, 1)
            dve.wait_ge(ids_loaded, 16 * G)
            for n, f in enumerate(SMALL_FIELDS):
                nc.vector.tensor_copy(ids16[:, :, n], ids_all[:, 0:TILES, f]).then_inc(small_consts, 1)
            nc.vector.memset(wide2[:, :, :], 0.0).then_inc(consts_ready, 1)

            set_diag(0)

            dve.wait_ge(w1_loaded, 32)
            lm = w1_rows[:, :].rearrange("p (l m) -> p l m", m=FIELDS)
            ml = w1_rows[:, :].rearrange("p (m l) -> p l m", l=FIELDS)
            for l0, n, wid, at in ((A0, NA, FIELDS, 0), (B0, NB_, WID_B, ROW_B), (C0, NC, NC, ROW_C)):
                m0 = FIELDS - wid
                nc.vector.tensor_tensor(
                    pair_w[:, at:at + n * wid].rearrange("p (l m) -> p l m", m=wid),
                    lm[:, l0:l0 + n, m0:FIELDS], ml[:, l0:l0 + n, m0:FIELDS], ALU.add).then_inc(pair_w_raw, 1)
            dve.wait_ge(pair_w_raw, 3)
            for l0, n, wid, at in ((A0, NA, FIELDS, 0), (B0, NB_, WID_B, ROW_B), (C0, NC, NC, ROW_C)):
                first = l0 * (FIELDS + 1)
                nc.vector.tensor_copy(pair_w[:, at:at + (wid + 1) * (n - 1) + 1:wid + 1],
                                      w1_rows[:, first:first + (FIELDS + 1) * (n - 1) + 1:FIELDS + 1]
                                      ).then_inc(pair_w_ready, 1)
            dve.wait_ge(pair_w_ready, 3)
            nc.vector.tensor_copy(sums[:, ONE, :], pair_w[:, :]).then_inc(wide_step, 1)
            steps = [1]

            def settle():
                dve.wait_ge(wide_step, steps[0])

            def step(ins):
                steps[0] += 1
                ins.then_inc(wide_step, 1)

            def make_weights():
                dve.wait_ge(ring_emptied, WIDE1_FROM)
                settle()

                def strided(first, stride, n, lo, num, by):
                    v = sums_flat[:, first:first + stride * n].rearrange("p (l x) -> p x l", x=stride)
                    return v[:, lo:lo + by * (num - 1) + 1:by, :]

                groups = (
                    (A0, NA, 0, FIELDS, [(B0, NB_ + NC, 0, FIELDS, B0, 1)]),
                    (B0, NB_, ROW_B, WID_B, [(A0, NA, B0, 1, 0, FIELDS), (C0, NC, ROW_B, WID_B, NB_, 1)]),
                    (C0, NC, ROW_C, NC, [(A0, NA, C0, 1, 0, FIELDS), (B0, NB_, ROW_B + NB_, 1, 0, WID_B)]),
                )
                for second in (False, True):
                    for l0, n, row, wid, others in groups:
                        for c0, num, base, per_l, lo, by in others:
                            for d in range(n - second):
                                e = d + second
                                at = pair_column(l0, e)
                                first = (l0 * W + per_l * e if second else (l0 + e) * W) + base
                                dst = wide1[:, c0:c0 + num, at:at + n - e]
                                step(nc.vector.tensor_tensor(
                                    dst, dst if second else pair_run(c0, num, row, wid, n, e),
                                    strided(first, W + per_l, n - e, lo, num, by), ALU.add))
                    settle()
                by_c = wide2[:, 0:NC, 0:CROSS].rearrange("p c (a b) -> p c a b", b=NB_)
                rows_a = sums[:, :, 0:ROW_B].rearrange("p j (l m) -> p j l m", m=FIELDS)
                rows_b = sums[:, :, ROW_B:ROW_C].rearrange("p j (l m) -> p j l m", m=WID_B)
                for c in range(NC):
                    step(nc.vector.tensor_tensor(
                        by_c[:, c], rows_a[:, C0 + c, :, B0:C0],
                        rows_a[:, B0:C0, :, C0 + c].rearrange("p b a -> p a b"), ALU.add))
                step(nc.vector.tensor_copy(wide2[:, 0:NC, CROSS], sums[:, C0:FIELDS, PAIRS]))
                step(nc.vector.tensor_copy(wide2[:, ONE2, RAW_AB:SECOND], sums[:, 0:C0, PAIRS]))
                w_a = pair_w[:, 0:ROW_B].rearrange("p (l m) -> p l m", m=FIELDS)
                w_b = pair_w[:, ROW_B:ROW_C].rearrange("p (l m) -> p l m", m=WID_B)
                step(nc.vector.tensor_copy(wide2[:, ONE1, 0:CROSS].rearrange("p (a b) -> p a b", b=NB_),
                                           w_a[:, :, B0:C0]))
                for c0, num, dst in (
                    (0, GRAM_FIELDS, wide2[:, SLOT_GRAM, 0:GRAM].rearrange("p (c l) -> p c l", l=MIXED)),
                    (GRAM_FIELDS, 1, wide2[:, ONE1, SECOND:ALL2].rearrange("p (c l) -> p c l", l=MIXED)),
                ):
                    step(nc.vector.tensor_copy(dst[:, :, 0:NA],
                                               w_a[:, :, C0 + c0:C0 + c0 + num].rearrange("p l c -> p c l")))
                    step(nc.vector.tensor_copy(dst[:, :, NA:MIXED],
                                               w_b[:, :, NB_ + c0:NB_ + c0 + num].rearrange("p l c -> p c l")))
                settle()
                for c in range(NC):
                    step(nc.vector.tensor_tensor(
                        by_c[:, c], by_c[:, c], rows_b[:, 0:NA, :, NB_ + c], ALU.add))
                settle()
                dve.wait_ge(small_loaded, 16 * 8)
                nc.vector.tensor_scalar(bias[:, :], bias[:, :], float(EMB), None, ALU.mult).then_inc(wide_ready, 1)

            def split_small():
                dve.wait_ge(small_rows_loaded, 16 * NSMALL)
                left = small_rows.rearrange("p (f a k) -> p f a k", f=NSMALL, a=PER_PART)
                for n in range(SPLITS):
                    nc.vector.tensor_copy(small_parts[:, :, :, n, :], left).then_inc(small_split, 1)
                    dve.wait_ge(small_split, 2 * n + 1)
                    if n < SPLITS - 1:
                        nc.vector.tensor_tensor(left, left, small_parts[:, :, :, n, :],
                                                ALU.subtract).then_inc(small_split, 1)
                        dve.wait_ge(small_split, 2 * n + 2)

            def split_dense():
                dve.wait_ge(dense_loaded, 16)
                at = 0
                for a in range(SPLITS):
                    num = sum(pair[0] == a for pair in DENSE_PAIRS)
                    nc.vector.tensor_copy(dense_parts[:, :, at:at + num, :],
                                          dense_rows[:, :, :].unsqueeze(2).broadcast_to([P, TILES, num, DENSE])
                                          ).then_inc(dense_split, 1)
                    dve.wait_ge(dense_split, 2 * a + 1)
                    if a < SPLITS - 1:
                        nc.vector.tensor_tensor(dense_rows[:, :, :], dense_rows[:, :, :], dense_parts[:, :, at, :],
                                                ALU.subtract).then_inc(dense_split, 1)
                        dve.wait_ge(dense_split, 2 * a + 2)
                    at += num

            def split_top():
                dve.wait_ge(small_loaded, 16 * 8)
                for b in range(SPLITS):
                    nc.vector.tensor_copy(top_parts[:, b, :], top1_dense[:, :]).then_inc(top_split, 1)
                    dve.wait_ge(top_split, 2 * b + 1)
                    if b < SPLITS - 1:
                        nc.vector.tensor_tensor(top1_dense[:, :], top1_dense[:, :], top_parts[:, b, :],
                                                ALU.subtract).then_inc(top_split, 1)
                        dve.wait_ge(top_split, 2 * b + 2)

            def find_rows(n):
                wait_for(dve, small_done, n - 1)
                for a in range(PER_PART):
                    nc.vector.tensor_scalar(onehot[n % 2][:, a, :, :].rearrange("p f n -> p (f n)"),
                                            ids_wide[:, n, :], row_of[0:SMALL_PARTS, a:a + 1], None,
                                            ALU.is_equal).then_inc(onehot_ready, 1)

            def add_parts(n):
                dve.wait_ge(small_done, n + 1)
                nc.vector.tensor_reduce(
                    found[:, n, :].rearrange("p (f k) -> p f k", f=NSMALL),
                    acc_first[n % 2][:, 0:NSMALL * SPLITS * EMB].rearrange(
                        "p (f s k) -> p f k s", f=NSMALL, s=SPLITS),
                    mybir.AxisListType.X, ALU.add).then_inc(small_copied, 1)

            def product_tile(i, q, first=False):
                dve.wait_ge(gathered[q], i * (16 * (FIELDS - NSMALL)) + 16 * FIELDS)
                dve.wait_ge(ids_padded, 1)
                nc.vector.tensor_copy(ids_now[:, q, :], ids_all[:, through(i, q, 1, TILES_PER_BLOCK), :]).then_inc(
                    ids_copied, 1)
                if not first:
                    n = i * TILES_PER_BLOCK + (q - FIRST_SMALL)
                    f = SMALL_FIELDS[0]
                    nc.vector.tensor_copy(rows[q][:, EMB * f:EMB * (f + NSMALL)],
                                          found[:, n, :]).then_inc(found_copied, 1)
                    dve.wait_ge(found_copied, n + 1)
                wait_for(dve, half_ready, i * (HALVES * HALF_STEPS) + 2 * q * HALF_STEPS)
                nc.vector.transpose(raw[:, :, :].rearrange("p t f -> p f t"),
                                    rows[q % 2][:, :].rearrange("p (f t) -> p f t", t=EMB)
                                    ).then_inc(raw_ready, 1)
                dve.wait_ge(raw_ready, i * TILES_PER_BLOCK + (q + 1))
                dve.sem_inc(rows_free, 1)
                for h in range(2):
                    x = raw[:, HALF * h:HALF * (h + 1), :]
                    ab = x[:, :, A0:C0].rearrange("p t (s l) -> p t s l", s=2)
                    half = 2 * q + h
                    dst = pairs[half]
                    wait_for(dve, triples_done, i * BANKS_PER_BLOCK + (BANKS_PER_HALF * (half + 1) - BANKS_PER_BLOCK))
                    for g in range(G):
                        lanes = slice(EMB * g, EMB * (g + 1))
                        nc.vector.tensor_copy(diag[half][lanes, :, 0:FIELDS, g], x[lanes]).then_inc(half_ready, 1)
                    nc.vector.tensor_copy(dst[:, :, WITHIN + RAW_AB:COLS], x[:, :, A0:C0]).then_inc(half_ready, 1)
                    for d in range(NA):
                        nc.vector.tensor_tensor(
                            dst[:, :, OFF_AB[d]:OFF_AB[d] + 2 * (NA - d)].rearrange("p t (s l) -> p t s l", s=2),
                            ab[:, :, :, 0:NA - d], ab[:, :, :, d:NA], ALU.mult).then_inc(half_ready, 1)
                    for d in range(NC):
                        nc.vector.tensor_tensor(
                            dst[:, :, OFF_C[d]:OFF_C[d] + NC - d],
                            x[:, :, C0:FIELDS - d], x[:, :, C0 + d:FIELDS], ALU.mult).then_inc(half_ready, 1)
                    nc.vector.tensor_tensor(
                        dst[:, :, WITHIN:WITHIN + CROSS].rearrange("p t (a b) -> p t a b", b=NB_),
                        x[:, :, A0:B0].unsqueeze(3).broadcast_to([P, HALF, NA, NB_]),
                        x[:, :, B0:C0].unsqueeze(2).broadcast_to([P, HALF, NA, NB_]),
                        ALU.mult).then_inc(half_ready, 1)

            split_small()
            dve.wait_ge(ring_emptied, W2_FROM)
            for n in range(SMALL_TILES + 1):
                if n < SMALL_TILES:
                    find_rows(n)
                if n >= 1:
                    add_parts(n - 1)
            dve.wait_ge(ring_filled, SUMS_FROM)
            set_ones(0)
            product_tile(0, 0, first=True)
            make_weights()
            dve.wait_ge(wide_own, OWN_COPIES)
            set_diag(2)
            set_ones(2)
            split_top()
            split_dense()
            product_tile(0, 1, first=True)
            with dve.Fori(1, BLOCKS) as i:
                for q in range(TILES_PER_BLOCK):
                    product_tile(i, q)

        @block.tensor
        def _(pe):
            pe.wait_ge(identity_ready, 1)

            def take_bank(n):
                if n >= len(ring):
                    pe.wait_ge(ring_emptied, n - len(ring) + 1)
                return ring[n % len(ring)]

            def look_up(n):
                pe.wait_ge(onehot_ready, (n + 1) * PER_PART)
                wait_for(pe, small_copied, n - 1)
                for f in range(NSMALL):
                    for a in range(PER_PART):
                        ins = nc.tensor.matmul(
                            acc_first[n % 2][:, SPLITS * EMB * f:SPLITS * EMB * (f + 1)], onehot[n % 2][:, a, f, :],
                            small_parts[:, f, a].rearrange("p s k -> p (s k)"),
                            start=(a == 0), stop=(a == PER_PART - 1))
                ins.then_inc(small_done, 1)

            pe.wait_ge(small_consts, 2 + NSMALL)
            for n, job in enumerate(ids_jobs):
                bank = take_bank(n)
                for x, t in enumerate(job):
                    for f in range(NSMALL):
                        at = P * (NSMALL * x + f)
                        ins = nc.tensor.matmul(
                            bank[0:SMALL_PARTS, at:at + P],
                            ids16[:, FIRST_SMALL + t, f:f + 1].broadcast_to([P, SMALL_PARTS]),
                            identity16[:, :], start=True, stop=True)
                ins.then_inc(ring_filled, 1)
            pe.wait_ge(w2_loaded, 16)
            for n, job in enumerate(w2_jobs):
                bank = take_bank(W2_FROM + n)
                for x, j in enumerate(job):
                    ins = nc.tensor.transpose(bank[:, P * x:P * (x + 1)], w2_rows[:, :, j], identity[:, :])
                ins.then_inc(ring_filled, 1)
            pe.wait_ge(pair_w_ready, 3)
            for j in range(FIELDS):
                bank = take_bank(SUMS_FROM + j)
                pe.wait_ge(ring_emptied, W2_FROM + j // 4 + 1)
                nc.tensor.matmul(bank[:, 0:W], w2_t[:, j, :], pair_w[:, :], start=True, stop=True).then_inc(
                    ring_filled, 1)
                if LOOK_UP_FROM <= j < LOOK_UP_FROM + SMALL_TILES:
                    look_up(j - LOOK_UP_FROM)
            def weights_by_feature():
                pe.wait_ge(wide_ready, 1)
                pe.wait_ge(wide_own, OWN_COPIES)
                for n, job in enumerate(wide1_jobs):
                    bank = take_bank(WIDE1_FROM + n)
                    for x, j in enumerate(job):
                        ins = nc.tensor.transpose(bank[0:WITHIN, P * x:P * (x + 1)], wide1[:, j, :], identity[:, :])
                    ins.then_inc(ring_filled, 1)
                for n, job in enumerate(wide2_jobs):
                    bank = take_bank(WIDE2_FROM + n)
                    for x, j in enumerate(job):
                        ins = nc.tensor.transpose(bank[0:GRAM, P * x:P * (x + 1)], wide2[:, j, :], identity[:, :])
                    ins.then_inc(ring_filled, 1)
                pe.wait_ge(ring_emptied, DENSE_FROM)
                pe.wait_ge(small_loaded, 16 * 8)

            def dense_by_feature():
                pe.wait_ge(dense_split, 2 * SPLITS - 1)
                pe.wait_ge(identity_b_ready, 1)
                for n, job in enumerate(dense_jobs):
                    if n >= 2:
                        pe.wait_ge(ring_emptied, DENSE_FROM + n - 1)
                    for x, t in enumerate(job):
                        ins = nc.tensor.matmul(acc_mlp[n % 2][:, P * x:P * (x + 1)],
                                               dense_parts[:, t, :, :].rearrange("p s d -> p (s d)"),
                                               identity_b[:, :], start=True, stop=True)
                    ins.then_inc(ring_filled, 1)

            def triple_banks(i, n):
                half, s = divmod(n, BANKS_PER_HALF)
                if s == 0:
                    pe.wait_ge(half_ready, i * (HALVES * HALF_STEPS) + HALF_STEPS * (half + 1))
                wait_for(pe, triples_copied, i * (2 * BANKS_PER_BLOCK) + 2 * (n - 1))
                for x in range(BANK_STEPS):
                    t = BANK_STEPS * s + x
                    nc.tensor.matmul(
                        acc_first[n % 2][0:WITHIN, FIELDS1 * G * x:FIELDS1 * G * (x + 1)],
                        pairs[half][:, t, 0:WITHIN],
                        diag[half][:, t, :, :].rearrange("p j g -> p (j g)"), start=True, stop=True)
                    ins = nc.tensor.matmul(
                        acc_second[n % 2][0:SECOND, SECOND_FIELDS * G * x:SECOND_FIELDS * G * (x + 1)],
                        pairs[half][:, t, WITHIN:COLS],
                        diag[half][:, t, SECOND_FROM:FIELDS1, :].rearrange("p j g -> p (j g)"),
                        start=True, stop=True)
                ins.then_inc(triples_done, 1)

            def layer_sums(i, q):
                cols = columns(q)
                pe.wait_ge(triples_copied, through(i, q + 1, 2 * BANKS_PER_TILE))
                for j in range(FIELDS):
                    nc.tensor.matmul(acc_z[1][:, cols], weights1[0:WITHIN, j, :], trip1[0:WITHIN, j, cols],
                                     start=(j == 0), stop=False)
                for c in range(NC):
                    nc.tensor.matmul(acc_z[1][:, cols], weights2[0:RAW_AB, c, :], trip2[0:RAW_AB, c, cols],
                                     start=False, stop=False)
                nc.tensor.matmul(acc_z[1][:, cols], weights2[0:SECOND, ONE2, :], trip2[0:SECOND, NC, cols],
                                 start=False, stop=True).then_inc(z_done, 1)
                pe.wait_ge(gram_ready, through(i, q + 1, 16 * NC))
                nc.tensor.matmul(acc_z[0][:, cols], weights1[0:WITHIN, ONE, :], trip1[0:WITHIN, ONE, cols],
                                 start=True, stop=False)
                nc.tensor.matmul(acc_z[0][:, cols], weights2[0:GRAM, SLOT_GRAM, :], gram[0:GRAM, cols],
                                 start=False, stop=False)
                nc.tensor.matmul(acc_z[0][:, cols], weights2[0:ALL2, ONE1, :], trip2[0:ALL2, NC, cols],
                                 start=False, stop=True).then_inc(z_done, 1)

            def mlp_result(i, q, r):
                cols = columns(q)
                def copied(n):
                    return through(i, q, RESULTS, n)

                acc = acc_mlp[r % 2]
                if r < RES1:
                    if r == 0:
                        pe.wait_ge(z_copied, through(i, q, 2, 2))
                    wait_for(pe, mlp_copied, copied(max(r - 1, 0)))
                    chunk = slice(P * r, P * (r + 1))
                    nc.tensor.matmul(acc[:, cols], top1[:, 0, chunk], z[:, 0, cols], start=True, stop=False)
                    nc.tensor.matmul(acc[:, cols], top1[:, 1, chunk], z[:, 1, cols], start=False, stop=False)
                    ins = nc.tensor.matmul(acc[:, cols], dense_w[:, chunk],
                                           dense_t[:, bass.ds(through(i, q, P), P)], start=False, stop=True)
                elif r < RES1 + RES2:
                    pe.wait_ge(mlp_copied, copied(RES1))
                    m = r - RES1
                    for k in range(RES1):
                        ins = nc.tensor.matmul(acc[:, cols], top2[:, k, P * m:P * (m + 1)], hid1[:, k, cols],
                                               start=(k == 0), stop=(k == RES1 - 1))
                else:
                    pe.wait_ge(mlp_copied, copied(RES1 + RES2))
                    for k in range(RES2):
                        ins = nc.tensor.matmul(acc[0:1, cols], top3[:, k:k + 1], hid2[:, k, cols],
                                               start=(k == 0), stop=(k == RES2 - 1))
                ins.then_inc(mlp_done, 1)

            def tile(i, q):
                for n in range(BANKS_PER_TILE):
                    triple_banks(i, BANKS_PER_TILE * q + n)
                    if n in MLP_AFTER:
                        if isinstance(i, int) and n == 0:
                            pe.wait_ge(ring_emptied, JOBS)
                            pe.wait_ge(dense_w_loaded, 16 * STACK)
                        mlp_result(i, q - 1, MLP_AFTER[n])
                layer_sums(i, q)
                mlp_result(i, q - 1, RESULTS - 1)

            pe.wait_ge(small_copied, SMALL_TILES)
            for n in range(BANKS_PER_TILE):
                triple_banks(0, n)
            weights_by_feature()
            layer_sums(0, 0)
            dense_by_feature()
            tile(0, 1)
            with pe.Fori(1, BLOCKS) as i:
                for q in range(TILES_PER_BLOCK):
                    tile(i, q)
            for r in range(RESULTS):
                mlp_result(BLOCKS, -1, r)

        @block.scalar
        def _(act):
            def filled(n):
                act.wait_ge(ring_filled, n + 1)
                return ring[n % len(ring)]

            for n, job in enumerate(ids_jobs):
                bank = filled(n)
                nc.scalar.copy(ids_wide[:, job[0]:job[-1] + 1, :],
                               bank[0:SMALL_PARTS, 0:NSMALL * P * len(job)].rearrange("p (t n) -> p t n", n=NSMALL * P)
                               ).then_inc(ring_emptied, 1)
            for n, job in enumerate(w2_jobs):
                bank = filled(W2_FROM + n)
                nc.scalar.copy(w2_t[:, job[0]:job[-1] + 1, :],
                               bank[:, 0:P * len(job)].rearrange("p (j h) -> p j h", h=P)).then_inc(ring_emptied, 1)
            for j in range(FIELDS):
                bank = filled(SUMS_FROM + j)
                nc.scalar.copy(sums[:, j, :], bank[:, 0:W]).then_inc(ring_emptied, 1)
            def weights_by_feature():
                for n, job in enumerate(wide1_jobs):
                    bank = filled(WIDE1_FROM + n)
                    nc.scalar.copy(weights1[0:WITHIN, job[0]:job[-1] + 1, :],
                                   bank[0:WITHIN, 0:P * len(job)].rearrange("p (j h) -> p j h", h=P)
                                   ).then_inc(ring_emptied, 1)
                for n, job in enumerate(wide2_jobs):
                    bank = filled(WIDE2_FROM + n)
                    nc.scalar.copy(weights2[0:GRAM, job[0]:job[-1] + 1, :],
                                   bank[0:GRAM, 0:P * len(job)].rearrange("p (j h) -> p j h", h=P)
                                   ).then_inc(ring_emptied, 1)
                act.wait_ge(small_loaded, 16 * 8)

            def dense_by_feature():
                for n in range(len(dense_jobs)):
                    act.wait_ge(ring_filled, DENSE_FROM + n + 1)
                    nc.scalar.copy(dense_t[:, 4 * P * n:4 * P * (n + 1)], acc_mlp[n % 2][:, :]).then_inc(ring_emptied, 1)

            def await_sums():
                act.wait_ge(small_done, SMALL_TILES)
                act.wait_ge(ring_emptied, WIDE1_FROM)
                act.wait_ge(wide_step, 1)

            def own_weights(d):
                for l0, n, row, wid in ((A0, NA, 0, FIELDS), (B0, NB_, ROW_B, WID_B), (C0, NC, ROW_C, NC)):
                    if d < n:
                        at = pair_column(l0, d)
                        for c0, num in ((l0, n), (ONE, 1)):
                            nc.scalar.copy(wide1[:, c0:c0 + num, at:at + n - d],
                                           pair_run(c0, num, row, wid, n, d)).then_inc(wide_own, 1)

            def copy_triples(i, n):
                q, first = divmod(n, BANKS_PER_TILE)
                if first == 0:
                    wait_for(act, z_done, through(i, q, 2, -2))
                act.wait_ge(triples_done, i * BANKS_PER_BLOCK + (n + 1))
                tokens = slice(BANK_STEPS * G * n, BANK_STEPS * G * (n + 1))
                nc.scalar.copy(
                    trip1[0:WITHIN, :, tokens].rearrange("p j (t g) -> p t j g", g=G),
                    acc_first[n % 2][0:WITHIN, 0:BANK_STEPS * FIELDS1 * G].rearrange(
                        "p (t j g) -> p t j g", j=FIELDS1, g=G)).then_inc(triples_copied, 1)
                nc.scalar.copy(
                    trip2[0:SECOND, :, tokens].rearrange("p j (t g) -> p t j g", g=G),
                    acc_second[n % 2][0:SECOND, 0:BANK_STEPS * SECOND_FIELDS * G].rearrange(
                        "p (t j g) -> p t j g", j=SECOND_FIELDS, g=G)[:, :, SECOND_FIELDS - KEPT:SECOND_FIELDS, :]
                ).then_inc(triples_copied, 1)

            def copy_sums(i, q):
                cols = columns(q)
                for n, m in enumerate((1, 0)):
                    act.wait_ge(z_done, through(i, q, 2, n + 1))
                    nc.scalar.activation(z[:, m, cols], acc_z[m][:, cols], ACT.Identity,
                                         bias=bias[:, m:m + 1]).then_inc(z_copied, 1)

            def copy_result(i, q, r):
                cols = columns(q)
                act.wait_ge(mlp_done, through(i, q, RESULTS, r + 1))
                if r < RES1:
                    ins = nc.scalar.activation(hid1[:, r, cols], acc_mlp[r % 2][:, cols], ACT.Relu,
                                               bias=bias_top1[:, r:r + 1])
                elif r < RES1 + RES2:
                    m = r - RES1
                    ins = nc.scalar.activation(hid2[:, m, cols], acc_mlp[r % 2][:, cols], ACT.Relu,
                                               bias=bias_top2[:, m:m + 1])
                else:
                    wait_for(act, y_stored, through(i, q, 16))
                    ins = nc.scalar.copy(y_now[:, cols], acc_mlp[r % 2][0:1, cols])
                ins.then_inc(mlp_copied, 1)

            def tile(i, q):
                for n in range(BANKS_PER_TILE):
                    copy_triples(i, BANKS_PER_TILE * q + n)
                    if n in MLP_AFTER:
                        copy_result(i, q - 1, MLP_AFTER[n])
                copy_sums(i, q)
                copy_result(i, q - 1, RESULTS - 1)

            await_sums()
            own_weights(0)
            for n in range(BANKS_PER_TILE):
                copy_triples(0, n)
                own_weights(n + 1)
            weights_by_feature()
            copy_sums(0, 0)
            dense_by_feature()
            tile(0, 1)
            with act.Fori(1, BLOCKS) as i:
                for q in range(TILES_PER_BLOCK):
                    tile(i, q)
            for r in range(RESULTS):
                copy_result(BLOCKS, -1, r)


_INS = (["dense_ctx", "ids"] + [f"tbl_{f}" for f in range(FIELDS)]
        + ["W_top1", "b_top1", "W_top2", "b_top2", "W_top3", "L0_rec_W1", "L0_rec_b1", "L0_rec_W2", "L0_rec_b2"])


def kernel(**inputs):
    import numpy as _np
    import concourse.bacc as _bacc
    from concourse import mybir as _mybir
    from concourse.bass_utils import run_bass_kernel_spmd as _run

    nc = _bacc.Bacc("TRN2", target_bir_lowering=False, num_devices=1)
    arrays, args = {}, []
    for name in _INS:
        a = _np.ascontiguousarray(inputs[name])
        arrays[f"in_{name}"] = a
        args.append(nc.dram_tensor(f"in_{name}", a.shape, _mybir.dt.from_np(a.dtype), kind="ExternalInput").ap())
    y = nc.dram_tensor("out_y", (TOKENS, 1), _mybir.dt.float32, kind="ExternalOutput").ap()
    build(nc, args[0], args[1], args[2:2 + FIELDS], *args[2 + FIELDS:], y)
    r = _run(nc, [arrays], core_ids=[0])
    return r.results[0]["out_y"]
```

```python
import concourse.bass as bass
from concourse import mybir
from contextlib import ExitStack

F32 = mybir.dt.float32
ALU = mybir.AluOpType
ACT = mybir.ActivationFunctionType

F16 = mybir.dt.float16
BF16 = mybir.dt.bfloat16

P = 128
TOKENS, FIELDS, EMB, DENSE = 2048, 26, 32, 16
H1, H2, TOP1, TOP2 = 128, 128, 512, 256
TILES = TOKENS // P
TILES_PER_BLOCK = 2
BLOCKS = TILES // TILES_PER_BLOCK
BLOCK = TILES_PER_BLOCK * P
G = P // EMB
STEPS = P // G
HALF = STEPS // 2
HALVES = 2 * TILES_PER_BLOCK
BANK_STEPS = 4
BANKS_PER_HALF = HALF // BANK_STEPS
BANKS_PER_TILE = 2 * BANKS_PER_HALF
BANKS_PER_BLOCK = TILES_PER_BLOCK * BANKS_PER_TILE

SMALL_FIELDS = (16, 17)
SMALL_ROWS = 1000
NSMALL = len(SMALL_FIELDS)
PER_PART = 8
SMALL_PARTS = SMALL_ROWS // PER_PART
SPLITS = 3
FIRST_SMALL = TILES_PER_BLOCK
SMALL_TILES = TILES - FIRST_SMALL
SMALL_BLOCKS = SMALL_TILES // TILES_PER_BLOCK

NA, NB_, NC = 9, 9, 8
A0, B0, C0 = 0, 9, 18
OFF_AB = [2 * sum(NA - x for x in range(d)) for d in range(NA)]
WITHIN_AB = NA * (NA + 1)
OFF_C = [WITHIN_AB + sum(NC - x for x in range(d)) for d in range(NC)]
WITHIN = WITHIN_AB + NC * (NC + 1) // 2
CROSS = NA * NB_
MIXED = NA + NB_
FIRST = WITHIN + 1
SECOND = CROSS + MIXED
COLS = FIRST + SECOND
ONE = FIELDS
FIELDS1 = FIELDS + 1
SECOND_FROM = 3
SECOND_FIELDS = FIELDS1 - SECOND_FROM
KEPT = NC + 1

ROW_B = NA * FIELDS
WID_B = FIELDS - B0
ROW_C = ROW_B + NB_ * WID_B
PAIRS = ROW_C + NC * NC
W = PAIRS + 1

GRAM_FIELDS = NC - 1
GRAM = GRAM_FIELDS * MIXED
ALL2 = SECOND + MIXED

ONE1, SLOT_GRAM = NC, NC + 1
SLOTS = NC + 2
FOLDED = 2
UNFOLDED = NC - FOLDED
SHARES = UNFOLDED // FOLDED
FOLD = CROSS // SHARES
FULL = SECOND + FOLD
assert FOLD * SHARES == CROSS and FULL <= GRAM

DENSE_PAIRS = [(a, b) for a in range(SPLITS) for b in range(SPLITS) if a + b < 2 * SPLITS - 2]
STACK = len(DENSE_PAIRS)


def build(nc, dense_ctx, ids, tables, w_top1, b_top1, w_top2, b_top2, w_top3, w1, b1, w2, b2, out):
    ctx = ExitStack()
    with ctx:
        def sb(name, shape, dt=F32):
            return ctx.enter_context(nc.sbuf_tensor(name, shape, dt))

        def sem(name):
            return ctx.enter_context(nc.semaphore(name))

        ids_all = sb("ids_all", [P, TILES + TILES_PER_BLOCK, FIELDS], mybir.dt.int32)
        ids_now = sb("ids_now", [P, TILES_PER_BLOCK, FIELDS], mybir.dt.int32)
        rows = [sb(f"rows{i}", [P, FIELDS * EMB]) for i in range(2)]
        raw = sb("raw", [P, STEPS, FIELDS])
        sums_flat = sb("sums", [P, FIELDS1 * W])
        sums = sums_flat[:, :].rearrange("p (j c) -> p j c", c=W)
        pairs = [sb(f"pairs{i}", [P, HALF, COLS])[:, :, :] for i in range(2)]
        diag = [sb(f"diag{i}", [P, HALF, FIELDS1, G])[:, :, :, :] for i in range(2)]
        at = 0
        for i in range(2):
            pairs.append(sums_flat[:, at:at + HALF * COLS].rearrange("p (t c) -> p t c", c=COLS))
            at += HALF * COLS
            diag.append(sums_flat[:, at:at + HALF * FIELDS1 * G].rearrange(
                "p (t j g) -> p t j g", j=FIELDS1, g=G))
            at += HALF * FIELDS1 * G
        trip1 = sb("trip1", [P, FIELDS1, BLOCK])
        trip2 = sb("trip2", [P, KEPT, BLOCK])
        top_parts = trip2[0:DENSE, :, :].rearrange("p j n -> p (j n)")[:, 0:SPLITS * TOP1 // 2].bitcast(
            BF16).rearrange("p (s n) -> p s n", n=TOP1)
        weights1 = sb("weights1", [P, FIELDS1, P])
        gram = sb("gram", [P, BLOCK])
        weights2 = sb("weights2", [P, SLOTS, P])
        pair_w = sb("pair_w", [P, W])
        w1_rows = sb("w1_rows", [P, FIELDS * FIELDS])
        identity = sb("identity", [P, P])
        top1 = sb("top1", [P, 2, TOP1])
        top1_dense = sb("top1_dense", [DENSE, TOP1])
        top2 = sb("top2", [P, TOP1 // P, TOP2])
        top3 = sb("top3", [P, TOP2 // P])
        bias = sb("bias", [P, 1])
        bias_top1 = sb("bias_top1", [P, TOP1 // P])
        bias_top2 = sb("bias_top2", [P, TOP2 // P])
        dense_rows = sb("dense_rows", [P, TILES, DENSE])
        late = sb("late", [P, max(FIELDS1 * FIRST, 8 * BLOCK)])
        z = late[:, 0:2 * BLOCK].rearrange("p (m n) -> p m n", n=BLOCK)
        hid1 = late[:, 2 * BLOCK:6 * BLOCK].rearrange("p (m n) -> p m n", n=BLOCK)
        hid2 = late[:, 6 * BLOCK:8 * BLOCK].rearrange("p (m n) -> p m n", n=BLOCK)
        wide1 = late[:, 0:FIELDS1 * FIRST].rearrange("p (j c) -> p j c", c=FIRST)
        wide2 = sb("wide2", [P, SLOTS, GRAM])
        w2_rows = pairs[1].rearrange("p t c -> p (t c)")[:, 0:H1 * FIELDS].rearrange(
            "p (i j) -> p i j", j=FIELDS)
        w2_t = weights1[:, 0:FIELDS, :]
        dense_all = sb("dense_all", [P, TOKENS])
        dense_t = dense_all[:, 0:TOKENS // 2].bitcast(BF16)
        dense_parts = dense_all[:, TOKENS // 2:TOKENS].bitcast(BF16).rearrange(
            "p (t s d) -> p t s d", s=STACK, d=DENSE)
        dense_w = sb("dense_w", [P, TOP1], BF16)
        identity_b = sb("identity_b", [P, P], BF16)
        y_now = sb("y_now", [1, BLOCK])
        found = sb("found", [P, SMALL_TILES, NSMALL * EMB])
        identity16 = sb("identity16", [P, P], F16)
        ids16 = sb("ids16", [P, TILES, NSMALL], F16)
        row_int = sb("row_int", [P, PER_PART], mybir.dt.int32)
        row_of = sb("row_of", [P, PER_PART])
        early = late[0:SMALL_PARTS, :]
        at = 0
        small_rows = early[:, at:at + NSMALL * PER_PART * EMB]
        at += NSMALL * PER_PART * EMB
        small_parts = early[:, at:at + NSMALL * PER_PART * SPLITS * EMB // 2].bitcast(BF16).rearrange(
            "p (f a s k) -> p f a s k", f=NSMALL, a=PER_PART, s=SPLITS)
        at += NSMALL * PER_PART * SPLITS * EMB // 2
        onehot = []
        for i in range(2):
            width = PER_PART * TILES_PER_BLOCK * NSMALL * P // 2
            onehot.append(trip1[0:SMALL_PARTS, :, :].rearrange("p j n -> p (j n)")[
                :, width * i:width * (i + 1)].bitcast(BF16).rearrange(
                "p (a q f n) -> p a q f n", q=TILES_PER_BLOCK, f=NSMALL, n=P))
        ids_wide = dense_all[0:SMALL_PARTS, 0:SMALL_TILES * NSMALL * P // 2].bitcast(F16).rearrange(
            "p (t n) -> p t n", n=NSMALL * P)

        acc_first = [ctx.enter_context(nc.psum_tensor(f"acc_first{i}", [P, 512], F32)) for i in range(2)]
        acc_second = [ctx.enter_context(nc.psum_tensor(f"acc_second{i}", [P, 512], F32)) for i in range(2)]
        acc_z = [ctx.enter_context(nc.psum_tensor(f"acc_z{i}", [P, 512], F32)) for i in range(2)]
        acc_mlp = [ctx.enter_context(nc.psum_tensor(f"acc_mlp{i}", [P, 512], F32)) for i in range(2)]
        ring = acc_z + acc_mlp

        ids_loaded = sem("ids_loaded")
        ids_copied = sem("ids_copied")
        ids_padded = sem("ids_padded")
        first_ids = sem("first_ids")
        w1_loaded = sem("w1_loaded")
        w2_loaded = sem("w2_loaded")
        dense_loaded = sem("dense_loaded")
        small_loaded = sem("small_loaded")
        identity_ready = sem("identity_ready")
        identity_ones = sem("identity_ones")
        identity_b_ready = sem("identity_b_ready")
        consts_ready = sem("consts_ready")
        pair_w_ready = sem("pair_w_ready")
        pair_w_raw = sem("pair_w_raw")
        ring_filled = sem("ring_filled")
        ring_emptied = sem("ring_emptied")
        wide_step = sem("wide_step")
        wide_ready = sem("wide_ready")
        wide_own = sem("wide_own")
        ones_ready = sem("ones_ready")
        dense_split = sem("dense_split")
        top_split = sem("top_split")
        dense_w_loaded = sem("dense_w_loaded")
        gathered = [sem(f"gathered{i}") for i in range(2)]
        tiles_begun = sem("tiles_begun")
        rows_free = sem("rows_free")
        raw_ready = sem("raw_ready")
        half_ready = sem("half_ready")
        triples_done = sem("triples_done")
        triples_copied = sem("triples_copied")
        row_int_ready = sem("row_int_ready")
        small_consts = sem("small_consts")
        small_rows_loaded = sem("small_rows_loaded")
        small_split = sem("small_split")
        onehot_ready = sem("onehot_ready")
        small_done = sem("small_done")
        small_copied = sem("small_copied")
        found_copied = sem("found_copied")
        gram_ready = sem("gram_ready")
        folded = sem("folded")
        z_done = sem("z_done")
        z_copied = sem("z_copied")
        mlp_done = sem("mlp_done")
        mlp_copied = sem("mlp_copied")
        y_stored = sem("y_stored")

        w2_jobs = [range(j, min(j + 4, FIELDS)) for j in range(0, FIELDS, 4)]
        dense_jobs = [range(t, t + 4) for t in range(0, TILES, 4)]
        wide1_jobs = [range(j, min(j + 4, FIELDS1)) for j in range(0, FIELDS1, 4)]
        wide2_jobs = [range(j, min(j + 4, SLOTS)) for j in range(0, SLOTS, 4)]
        per_bank = 512 // (NSMALL * P)
        ids_jobs = [range(t, min(t + per_bank, SMALL_TILES)) for t in range(0, SMALL_TILES, per_bank)]
        W2_FROM = len(ids_jobs)
        SUMS_FROM = W2_FROM + len(w2_jobs)
        WIDE1_FROM = SUMS_FROM + FIELDS
        WIDE2_FROM = WIDE1_FROM + len(wide1_jobs)
        DENSE_FROM = WIDE2_FROM + len(wide2_jobs)
        JOBS = DENSE_FROM + len(dense_jobs)
        MLP_AFTER = {2: 0, 3: 1, 4: 2, 5: 3, 6: 4, BANKS_PER_TILE - 1: 5}
        assert NA == BANKS_PER_TILE + 1
        LOOK_UP_AFTER = [1 + 8 * n // 5 for n in range(SMALL_BLOCKS)]
        RES1, RES2 = TOP1 // P, TOP2 // P
        RESULTS = RES1 + RES2 + 1
        SMALL_LOADS = 7
        OWN_COPIES = 2 * (NA + NB_ + NC)

        HALF_STEPS = G + 1 + NA + NC + 1

        def pair_column(l0, d):
            return OFF_C[d] if l0 == C0 else OFF_AB[d] + (NB_ - d) * (l0 == B0)

        def pair_run(c0, num, row, wid, n, d):
            return sums[:, c0:c0 + num, row + d:row + d + (wid + 1) * (n - d - 1) + 1:wid + 1]

        def through(i, q, each, more=0):
            return i * (TILES_PER_BLOCK * each) + (q * each + more)

        def columns(q):
            q %= TILES_PER_BLOCK
            return slice(P * q, P * (q + 1))

        def wait_for(eng, semaphore, value):
            if not isinstance(value, int) or value > 0:
                eng.wait_ge(semaphore, value)

        block = ctx.enter_context(nc.Block())

        @block.sync
        def _(sp):
            by_lane = ids.rearrange("(n t g) f -> g t n f", g=G, t=STEPS)
            for g in range(G):
                sp.dma_start(ids_all[EMB * g:EMB * (g + 1), 0:TILES, :], by_lane[g]).then_inc(ids_loaded, 16)
            for n, f in enumerate(SMALL_FIELDS):
                sp.dma_start(small_rows[:, PER_PART * EMB * n:PER_PART * EMB * (n + 1)],
                             tables[f].rearrange("(p a) k -> p (a k)", a=PER_PART)).then_inc(small_rows_loaded, 16)
            sp.dma_start(w2_rows, w2).then_inc(w2_loaded, 16)
            sp.dma_start(w1_rows[:, :], w1.rearrange("i l m -> i (l m)")).then_inc(w1_loaded, 16)
            sp.dma_start(pair_w[:, PAIRS:W], b1.rearrange("(p o) -> p o", o=1)).then_inc(w1_loaded, 16)
            sp.dma_start(dense_rows[:, :, :], dense_ctx.rearrange("(n p) d -> p n d", p=P)).then_inc(
                dense_loaded, 16)
            for dst, src in (
                (bias[:, 0:1], b2.rearrange("(p o) -> p o", o=1)),
                (bias_top1[:, :], b_top1.rearrange("(m p) -> p m", p=P)),
                (bias_top2[:, :], b_top2.rearrange("(m p) -> p m", p=P)),
                (top3[:, :], w_top3.rearrange("(m p) o -> p (m o)", p=P)),
                (top1[:, :, :], w_top1[0:H1 + H2, :].rearrange("(m p) n -> p m n", p=P)),
                (top1_dense[:, :], w_top1[H1 + H2:H1 + H2 + DENSE, :]),
                (top2[:, :, :], w_top2.rearrange("(m p) n -> p m n", p=P)),
            ):
                sp.dma_start(dst, src, allow_slow_non_contiguous=True).then_inc(small_loaded, 16)
            sp.wait_ge(top_split, 2 * SPLITS - 1)
            for n, (_a, b) in enumerate(DENSE_PAIRS):
                sp.dma_start(dense_w[DENSE * n:DENSE * (n + 1), :], top_parts[:, b, :]).then_inc(dense_w_loaded, 16)

            def store_y(t):
                sp.wait_ge(mlp_copied, (t + 1) * RESULTS)
                sp.dma_start(out.rearrange("n o -> o n")[:, P * t:P * (t + 1)],
                             y_now[:, columns(t)]).then_inc(y_stored, 16)

            for t in range(TILES):
                cols = columns(t)
                sp.wait_ge(triples_copied, 2 * BANKS_PER_TILE * (t + 1))
                for n in range(FOLDED if t < TILES - 1 else 0):
                    for x in range(SHARES):
                        sp.dma_start(trip2[SECOND:FULL, SHARES * n + x, cols],
                                     trip2[FOLD * x:FOLD * (x + 1), UNFOLDED + n, cols]).then_inc(folded, 16)
                for c in range(GRAM_FIELDS):
                    sp.dma_start(gram[MIXED * c:MIXED * (c + 1), cols],
                                 trip2[CROSS:SECOND, c, cols]).then_inc(gram_ready, 16)
                sp.dma_start(trip2[SECOND:ALL2, NC, cols],
                             trip2[CROSS:SECOND, NC - 1, cols]).then_inc(gram_ready, 16)
                if t > 0:
                    store_y(t - 1)
            store_y(TILES - 1)
            sp.wait_ge(y_stored, 16 * TILES)

        @block.gpsimd
        def _(pool):
            nc.gpsimd.memset(identity[:, :], 1.0).then_inc(identity_ones, 1)
            pool.wait_ge(identity_ones, 1)
            nc.gpsimd.affine_select(out=identity[:, :], in_=identity[:, :], compare_op=ALU.is_equal,
                                    fill=0.0, base=0, pattern=[[-1, P]],
                                    channel_multiplier=1).then_inc(identity_ready, 1)
            nc.gpsimd.iota(row_int[:, :], pattern=[[1, PER_PART]], base=0,
                           channel_multiplier=PER_PART).then_inc(row_int_ready, 1)
            pool.wait_ge(ids_loaded, 16 * G)

            def gather_block(i, fields):
                for q in range(TILES_PER_BLOCK):
                    wait_for(pool, rows_free, through(i, q, 1, -1))
                    if isinstance(i, int):
                        pool.wait_ge(first_ids, q + 1)
                    else:
                        pool.wait_ge(ids_copied, through(i, q, 1, -1))
                    pool.sem_inc(tiles_begun, 1)
                    for f in fields:
                        nc.gpsimd.indirect_dma_start(
                            out=rows[q % 2][:, EMB * f:EMB * (f + 1)], out_offset=None, in_=tables[f],
                            in_offset=bass.IndirectOffsetOnAxis(ids_now[:, q, f:f + 1], 0),
                        ).then_inc(gathered[q % 2], 16)

            for q in range(TILES_PER_BLOCK):
                nc.gpsimd.tensor_copy(ids_now[:, q, :], ids_all[:, q, :]).then_inc(first_ids, 1)
            gather_block(0, range(FIELDS))
            with pool.Fori(1, BLOCKS) as i:
                gather_block(i, [f for f in range(FIELDS) if f not in SMALL_FIELDS])

        @block.vector
        def _(dve):
            def set_diag(n):
                for h in (n, n + 1):
                    nc.vector.memset(diag[h], 0.0).then_inc(consts_ready, 1)
                dve.wait_ge(consts_ready, 1 + n * (1 + G) + 2)
                for h in (n, n + 1):
                    for g in range(G):
                        nc.vector.memset(diag[h][EMB * g:EMB * (g + 1), :, ONE, g], 1.0).then_inc(consts_ready, 1)
                dve.wait_ge(consts_ready, 1 + (n + 2) * (1 + G))

            def set_ones(n):
                for h in (n, n + 1):
                    nc.vector.memset(pairs[h][:, :, WITHIN:FIRST], 1.0).then_inc(ones_ready, 1)
                dve.wait_ge(ones_ready, n + 2)

            dve.wait_ge(row_int_ready, 1)
            nc.vector.tensor_copy(row_of[:, :], row_int[:, :]).then_inc(small_consts, 1)
            dve.wait_ge(identity_ready, 1)
            nc.vector.tensor_copy(identity16[:, :], identity[:, :]).then_inc(small_consts, 1)
            nc.vector.tensor_copy(identity_b[:, :], identity[:, :]).then_inc(identity_b_ready, 1)
            nc.vector.memset(ids_all[:, TILES:TILES + TILES_PER_BLOCK, :], 0).then_inc(ids_padded, 1)
            dve.wait_ge(ids_loaded, 16 * G)
            for n, f in enumerate(SMALL_FIELDS):
                nc.vector.tensor_copy(ids16[:, :, n], ids_all[:, 0:TILES, f]).then_inc(small_consts, 1)
            nc.vector.memset(wide2[:, :, :], 0.0).then_inc(consts_ready, 1)

            set_diag(0)

            dve.wait_ge(w1_loaded, 32)
            lm = w1_rows[:, :].rearrange("p (l m) -> p l m", m=FIELDS)
            ml = w1_rows[:, :].rearrange("p (m l) -> p l m", l=FIELDS)
            for l0, n, wid, at in ((A0, NA, FIELDS, 0), (B0, NB_, WID_B, ROW_B), (C0, NC, NC, ROW_C)):
                m0 = FIELDS - wid
                nc.vector.tensor_tensor(
                    pair_w[:, at:at + n * wid].rearrange("p (l m) -> p l m", m=wid),
                    lm[:, l0:l0 + n, m0:FIELDS], ml[:, l0:l0 + n, m0:FIELDS], ALU.add).then_inc(pair_w_raw, 1)
            dve.wait_ge(pair_w_raw, 3)
            for l0, n, wid, at in ((A0, NA, FIELDS, 0), (B0, NB_, WID_B, ROW_B), (C0, NC, NC, ROW_C)):
                first = l0 * (FIELDS + 1)
                nc.vector.tensor_copy(pair_w[:, at:at + (wid + 1) * (n - 1) + 1:wid + 1],
                                      w1_rows[:, first:first + (FIELDS + 1) * (n - 1) + 1:FIELDS + 1]
                                      ).then_inc(pair_w_ready, 1)
            dve.wait_ge(pair_w_ready, 3)
            nc.vector.tensor_copy(sums[:, ONE, :], pair_w[:, :]).then_inc(wide_step, 1)
            steps = [1]

            def settle():
                dve.wait_ge(wide_step, steps[0])

            def step(ins):
                steps[0] += 1
                ins.then_inc(wide_step, 1)

            def make_weights():
                dve.wait_ge(ring_emptied, WIDE1_FROM)
                settle()

                def strided(first, stride, n, lo, num, by):
                    v = sums_flat[:, first:first + stride * n].rearrange("p (l x) -> p x l", x=stride)
                    return v[:, lo:lo + by * (num - 1) + 1:by, :]

                groups = (
                    (A0, NA, 0, FIELDS, [(B0, NB_ + NC, 0, FIELDS, B0, 1)]),
                    (B0, NB_, ROW_B, WID_B, [(A0, NA, B0, 1, 0, FIELDS), (C0, NC, ROW_B, WID_B, NB_, 1)]),
                    (C0, NC, ROW_C, NC, [(A0, NA, C0, 1, 0, FIELDS), (B0, NB_, ROW_B + NB_, 1, 0, WID_B)]),
                )
                for second in (False, True):
                    for l0, n, row, wid, others in groups:
                        for c0, num, base, per_l, lo, by in others:
                            for d in range(n - second):
                                e = d + second
                                at = pair_column(l0, e)
                                first = (l0 * W + per_l * e if second else (l0 + e) * W) + base
                                dst = wide1[:, c0:c0 + num, at:at + n - e]
                                step(nc.vector.tensor_tensor(
                                    dst, dst if second else pair_run(c0, num, row, wid, n, e),
                                    strided(first, W + per_l, n - e, lo, num, by), ALU.add))
                    settle()
                by_c = wide2[:, 0:NC, 0:CROSS].rearrange("p c (a b) -> p c a b", b=NB_)
                rows_a = sums[:, :, 0:ROW_B].rearrange("p j (l m) -> p j l m", m=FIELDS)
                rows_b = sums[:, :, ROW_B:ROW_C].rearrange("p j (l m) -> p j l m", m=WID_B)
                for c in range(NC):
                    step(nc.vector.tensor_tensor(
                        by_c[:, c], rows_a[:, C0 + c, :, B0:C0],
                        rows_a[:, B0:C0, :, C0 + c].rearrange("p b a -> p a b"), ALU.add))
                step(nc.vector.tensor_copy(wide1[:, :, WITHIN], sums[:, :, PAIRS]))
                w_a = pair_w[:, 0:ROW_B].rearrange("p (l m) -> p l m", m=FIELDS)
                w_b = pair_w[:, ROW_B:ROW_C].rearrange("p (l m) -> p l m", m=WID_B)
                step(nc.vector.tensor_copy(wide2[:, ONE1, 0:CROSS].rearrange("p (a b) -> p a b", b=NB_),
                                           w_a[:, :, B0:C0]))
                for c0, num, dst in (
                    (0, GRAM_FIELDS, wide2[:, SLOT_GRAM, 0:GRAM].rearrange("p (c l) -> p c l", l=MIXED)),
                    (GRAM_FIELDS, 1, wide2[:, ONE1, SECOND:ALL2].rearrange("p (c l) -> p c l", l=MIXED)),
                ):
                    step(nc.vector.tensor_copy(dst[:, :, 0:NA],
                                               w_a[:, :, C0 + c0:C0 + c0 + num].rearrange("p l c -> p c l")))
                    step(nc.vector.tensor_copy(dst[:, :, NA:MIXED],
                                               w_b[:, :, NB_ + c0:NB_ + c0 + num].rearrange("p l c -> p c l")))
                settle()
                for c in range(NC):
                    step(nc.vector.tensor_tensor(
                        by_c[:, c], by_c[:, c], rows_b[:, 0:NA, :, NB_ + c], ALU.add))
                settle()
                for n in range(FOLDED):
                    step(nc.vector.tensor_copy(
                        wide2[:, SHARES * n:SHARES * (n + 1), SECOND:FULL],
                        wide2[:, UNFOLDED + n, 0:CROSS].rearrange("p (x r) -> p x r", r=FOLD)))
                settle()
                dve.wait_ge(small_loaded, 16 * SMALL_LOADS)
                nc.vector.tensor_scalar(bias[:, :], bias[:, :], float(EMB), None, ALU.mult).then_inc(wide_ready, 1)

            def split_small():
                dve.wait_ge(small_rows_loaded, 16 * NSMALL)
                left = small_rows.rearrange("p (f a k) -> p f a k", f=NSMALL, a=PER_PART)
                for n in range(SPLITS):
                    nc.vector.tensor_copy(small_parts[:, :, :, n, :], left).then_inc(small_split, 1)
                    dve.wait_ge(small_split, 2 * n + 1)
                    if n < SPLITS - 1:
                        nc.vector.tensor_tensor(left, left, small_parts[:, :, :, n, :],
                                                ALU.subtract).then_inc(small_split, 1)
                        dve.wait_ge(small_split, 2 * n + 2)

            def split_dense():
                dve.wait_ge(dense_loaded, 16)
                at = 0
                for a in range(SPLITS):
                    num = sum(pair[0] == a for pair in DENSE_PAIRS)
                    nc.vector.tensor_copy(dense_parts[:, :, at:at + num, :],
                                          dense_rows[:, :, :].unsqueeze(2).broadcast_to([P, TILES, num, DENSE])
                                          ).then_inc(dense_split, 1)
                    dve.wait_ge(dense_split, 2 * a + 1)
                    if a < SPLITS - 1:
                        nc.vector.tensor_tensor(dense_rows[:, :, :], dense_rows[:, :, :], dense_parts[:, :, at, :],
                                                ALU.subtract).then_inc(dense_split, 1)
                        dve.wait_ge(dense_split, 2 * a + 2)
                    at += num

            def split_top():
                dve.wait_ge(small_loaded, 16 * SMALL_LOADS)
                for b in range(SPLITS):
                    nc.vector.tensor_copy(top_parts[:, b, :], top1_dense[:, :]).then_inc(top_split, 1)
                    dve.wait_ge(top_split, 2 * b + 1)
                    if b < SPLITS - 1:
                        nc.vector.tensor_tensor(top1_dense[:, :], top1_dense[:, :], top_parts[:, b, :],
                                                ALU.subtract).then_inc(top_split, 1)
                        dve.wait_ge(top_split, 2 * b + 2)

            def find_rows(n):
                wait_for(dve, small_done, n - 1)
                for a in range(PER_PART):
                    nc.vector.tensor_scalar(
                        onehot[n % 2][:, a].rearrange("p q f n -> p (q f n)"),
                        ids_wide[:, TILES_PER_BLOCK * n:TILES_PER_BLOCK * (n + 1), :].rearrange("p q n -> p (q n)"),
                        row_of[0:SMALL_PARTS, a:a + 1], None, ALU.is_equal).then_inc(onehot_ready, 1)

            def add_parts(n):
                dve.wait_ge(small_done, n + 1)
                nc.vector.tensor_reduce(
                    found[:, TILES_PER_BLOCK * n:TILES_PER_BLOCK * (n + 1), :].rearrange(
                        "p q (f k) -> p (q f) k", f=NSMALL),
                    acc_first[n % 2][:, 0:TILES_PER_BLOCK * NSMALL * SPLITS * EMB].rearrange(
                        "p (x s k) -> p x k s", s=SPLITS, k=EMB),
                    mybir.AxisListType.X, ALU.add).then_inc(small_copied, 1)

            def product_tile(i, q, first=False):
                dve.wait_ge(gathered[q], i * (16 * (FIELDS - NSMALL)) + 16 * FIELDS)
                dve.wait_ge(ids_padded, 1)
                nc.vector.tensor_copy(ids_now[:, q, :], ids_all[:, through(i, q, 1, TILES_PER_BLOCK), :]).then_inc(
                    ids_copied, 1)
                if not first:
                    n = i * TILES_PER_BLOCK + (q - FIRST_SMALL)
                    f = SMALL_FIELDS[0]
                    nc.vector.tensor_copy(rows[q][:, EMB * f:EMB * (f + NSMALL)],
                                          found[:, n, :]).then_inc(found_copied, 1)
                    dve.wait_ge(found_copied, n + 1)
                wait_for(dve, half_ready, i * (HALVES * HALF_STEPS) + 2 * q * HALF_STEPS)
                nc.vector.transpose(raw[:, :, :].rearrange("p t f -> p f t"),
                                    rows[q % 2][:, :].rearrange("p (f t) -> p f t", t=EMB)
                                    ).then_inc(raw_ready, 1)
                dve.wait_ge(raw_ready, i * TILES_PER_BLOCK + (q + 1))
                dve.sem_inc(rows_free, 1)
                for h in range(2):
                    x = raw[:, HALF * h:HALF * (h + 1), :]
                    ab = x[:, :, A0:C0].rearrange("p t (s l) -> p t s l", s=2)
                    half = 2 * q + h
                    dst = pairs[half]
                    wait_for(dve, triples_done, i * BANKS_PER_BLOCK + (BANKS_PER_HALF * (half + 1) - BANKS_PER_BLOCK))
                    for g in range(G):
                        lanes = slice(EMB * g, EMB * (g + 1))
                        nc.vector.tensor_copy(diag[half][lanes, :, 0:FIELDS, g], x[lanes]).then_inc(half_ready, 1)
                    nc.vector.tensor_copy(dst[:, :, FIRST + CROSS:COLS], x[:, :, A0:C0]).then_inc(half_ready, 1)
                    for d in range(NA):
                        nc.vector.tensor_tensor(
                            dst[:, :, OFF_AB[d]:OFF_AB[d] + 2 * (NA - d)].rearrange("p t (s l) -> p t s l", s=2),
                            ab[:, :, :, 0:NA - d], ab[:, :, :, d:NA], ALU.mult).then_inc(half_ready, 1)
                    for d in range(NC):
                        nc.vector.tensor_tensor(
                            dst[:, :, OFF_C[d]:OFF_C[d] + NC - d],
                            x[:, :, C0:FIELDS - d], x[:, :, C0 + d:FIELDS], ALU.mult).then_inc(half_ready, 1)
                    nc.vector.tensor_tensor(
                        dst[:, :, FIRST:FIRST + CROSS].rearrange("p t (a b) -> p t a b", b=NB_),
                        x[:, :, A0:B0].unsqueeze(3).broadcast_to([P, HALF, NA, NB_]),
                        x[:, :, B0:C0].unsqueeze(2).broadcast_to([P, HALF, NA, NB_]),
                        ALU.mult).then_inc(half_ready, 1)

            split_small()
            dve.wait_ge(ring_emptied, W2_FROM)
            for n in range(SMALL_BLOCKS + 1):
                if n < SMALL_BLOCKS:
                    find_rows(n)
                else:
                    split_top()
                if n >= 1:
                    add_parts(n - 1)
            dve.wait_ge(ring_filled, SUMS_FROM)
            set_ones(0)
            product_tile(0, 0, first=True)
            make_weights()
            dve.wait_ge(wide_own, OWN_COPIES)
            set_diag(2)
            set_ones(2)
            split_dense()
            product_tile(0, 1, first=True)
            with dve.Fori(1, BLOCKS) as i:
                for q in range(TILES_PER_BLOCK):
                    product_tile(i, q)

        @block.tensor
        def _(pe):
            pe.wait_ge(identity_ready, 1)

            def take_bank(n):
                if n >= len(ring):
                    pe.wait_ge(ring_emptied, n - len(ring) + 1)
                return ring[n % len(ring)]

            def look_up(n):
                pe.wait_ge(onehot_ready, (n + 1) * PER_PART)
                wait_for(pe, small_copied, n - 1)
                for q in range(TILES_PER_BLOCK):
                    for f in range(NSMALL):
                        at = SPLITS * EMB * (NSMALL * q + f)
                        for a in range(PER_PART):
                            ins = nc.tensor.matmul(
                                acc_first[n % 2][:, at:at + SPLITS * EMB], onehot[n % 2][:, a, q, f, :],
                                small_parts[:, f, a].rearrange("p s k -> p (s k)"),
                                start=(a == 0), stop=(a == PER_PART - 1))
                ins.then_inc(small_done, 1)

            pe.wait_ge(small_consts, 2 + NSMALL)
            for n, job in enumerate(ids_jobs):
                bank = take_bank(n)
                for x, t in enumerate(job):
                    for f in range(NSMALL):
                        at = P * (NSMALL * x + f)
                        ins = nc.tensor.matmul(
                            bank[0:SMALL_PARTS, at:at + P],
                            ids16[:, FIRST_SMALL + t, f:f + 1].broadcast_to([P, SMALL_PARTS]),
                            identity16[:, :], start=True, stop=True)
                ins.then_inc(ring_filled, 1)
            pe.wait_ge(w2_loaded, 16)
            for n, job in enumerate(w2_jobs):
                bank = take_bank(W2_FROM + n)
                for x, j in enumerate(job):
                    ins = nc.tensor.transpose(bank[:, P * x:P * (x + 1)], w2_rows[:, :, j], identity[:, :])
                ins.then_inc(ring_filled, 1)
            pe.wait_ge(pair_w_ready, 3)
            for j in range(FIELDS):
                bank = take_bank(SUMS_FROM + j)
                pe.wait_ge(ring_emptied, W2_FROM + j // 4 + 1)
                nc.tensor.matmul(bank[:, 0:W], w2_t[:, j, :], pair_w[:, :], start=True, stop=True).then_inc(
                    ring_filled, 1)
                if j in LOOK_UP_AFTER:
                    look_up(LOOK_UP_AFTER.index(j))

            def weights_by_feature():
                pe.wait_ge(wide_ready, 1)
                pe.wait_ge(wide_own, OWN_COPIES)
                for n, job in enumerate(wide1_jobs):
                    bank = take_bank(WIDE1_FROM + n)
                    for x, j in enumerate(job):
                        ins = nc.tensor.transpose(bank[0:FIRST, P * x:P * (x + 1)], wide1[:, j, :], identity[:, :])
                    ins.then_inc(ring_filled, 1)
                for n, job in enumerate(wide2_jobs):
                    bank = take_bank(WIDE2_FROM + n)
                    for x, j in enumerate(job):
                        ins = nc.tensor.transpose(bank[0:GRAM, P * x:P * (x + 1)], wide2[:, j, :], identity[:, :])
                    ins.then_inc(ring_filled, 1)
                pe.wait_ge(ring_emptied, DENSE_FROM)
                pe.wait_ge(small_loaded, 16 * SMALL_LOADS)

            def dense_by_feature():
                pe.wait_ge(dense_split, 2 * SPLITS - 1)
                pe.wait_ge(identity_b_ready, 1)
                for n, job in enumerate(dense_jobs):
                    if n >= 2:
                        pe.wait_ge(ring_emptied, DENSE_FROM + n - 1)
                    for x, t in enumerate(job):
                        ins = nc.tensor.matmul(acc_mlp[n % 2][:, P * x:P * (x + 1)],
                                               dense_parts[:, t, :, :].rearrange("p s d -> p (s d)"),
                                               identity_b[:, :], start=True, stop=True)
                    ins.then_inc(ring_filled, 1)

            def triple_banks(i, n):
                half, s = divmod(n, BANKS_PER_HALF)
                if s == 0:
                    pe.wait_ge(half_ready, i * (HALVES * HALF_STEPS) + HALF_STEPS * (half + 1))
                wait_for(pe, triples_copied, i * (2 * BANKS_PER_BLOCK) + 2 * (n - 1))
                for x in range(BANK_STEPS):
                    t = BANK_STEPS * s + x
                    nc.tensor.matmul(
                        acc_first[n % 2][0:FIRST, FIELDS1 * G * x:FIELDS1 * G * (x + 1)],
                        pairs[half][:, t, 0:FIRST],
                        diag[half][:, t, :, :].rearrange("p j g -> p (j g)"), start=True, stop=True)
                    ins = nc.tensor.matmul(
                        acc_second[n % 2][0:SECOND, SECOND_FIELDS * G * x:SECOND_FIELDS * G * (x + 1)],
                        pairs[half][:, t, FIRST:COLS],
                        diag[half][:, t, SECOND_FROM:FIELDS1, :].rearrange("p j g -> p (j g)"),
                        start=True, stop=True)
                ins.then_inc(triples_done, 1)

            def sum_triples(i, q):
                cols = columns(q)
                pe.wait_ge(triples_copied, through(i, q + 1, 2 * BANKS_PER_TILE))
                for j in range(FIELDS):
                    nc.tensor.matmul(acc_z[1][:, cols], weights1[0:FIRST, j, :], trip1[0:FIRST, j, cols],
                                     start=(j == 0), stop=False)

            def sum_cross(i, q):
                cols = columns(q)
                pe.wait_ge(folded, through(i, q + 1, 16 * FOLDED * SHARES))
                for c in range(UNFOLDED):
                    ins = nc.tensor.matmul(acc_z[1][:, cols], weights2[0:FULL, c, :], trip2[0:FULL, c, cols],
                                           start=False, stop=(c == UNFOLDED - 1))
                ins.then_inc(z_done, 1)

            def sum_cross_unfolded():
                cols = columns(-1)
                for c in range(NC):
                    ins = nc.tensor.matmul(acc_z[1][:, cols], weights2[0:CROSS, c, :], trip2[0:CROSS, c, cols],
                                           start=False, stop=(c == NC - 1))
                ins.then_inc(z_done, 1)

            def sum_pairs(i, q):
                cols = columns(q)
                pe.wait_ge(gram_ready, through(i, q + 1, 16 * NC))
                nc.tensor.matmul(acc_z[0][:, cols], weights1[0:FIRST, ONE, :], trip1[0:FIRST, ONE, cols],
                                 start=True, stop=False)
                nc.tensor.matmul(acc_z[0][:, cols], weights2[0:GRAM, SLOT_GRAM, :], gram[0:GRAM, cols],
                                 start=False, stop=False)
                nc.tensor.matmul(acc_z[0][:, cols], weights2[0:ALL2, ONE1, :], trip2[0:ALL2, NC, cols],
                                 start=False, stop=True).then_inc(z_done, 1)

            def mlp_result(i, q, r):
                cols = columns(q)

                def copied(n):
                    return through(i, q, RESULTS, n)

                acc = acc_mlp[r % 2]
                if r < RES1:
                    if r == 0:
                        pe.wait_ge(z_copied, through(i, q, 2, 2))
                    wait_for(pe, mlp_copied, copied(max(r - 1, 0)))
                    chunk = slice(P * r, P * (r + 1))
                    nc.tensor.matmul(acc[:, cols], top1[:, 0, chunk], z[:, 0, cols], start=True, stop=False)
                    nc.tensor.matmul(acc[:, cols], top1[:, 1, chunk], z[:, 1, cols], start=False, stop=False)
                    ins = nc.tensor.matmul(acc[:, cols], dense_w[:, chunk],
                                           dense_t[:, bass.ds(through(i, q, P), P)], start=False, stop=True)
                elif r < RES1 + RES2:
                    pe.wait_ge(mlp_copied, copied(RES1))
                    m = r - RES1
                    for k in range(RES1):
                        ins = nc.tensor.matmul(acc[:, cols], top2[:, k, P * m:P * (m + 1)], hid1[:, k, cols],
                                               start=(k == 0), stop=(k == RES1 - 1))
                else:
                    pe.wait_ge(mlp_copied, copied(RES1 + RES2))
                    for k in range(RES2):
                        ins = nc.tensor.matmul(acc[0:1, cols], top3[:, k:k + 1], hid2[:, k, cols],
                                               start=(k == 0), stop=(k == RES2 - 1))
                ins.then_inc(mlp_done, 1)

            def tile(i, q):
                for n in range(BANKS_PER_TILE):
                    triple_banks(i, BANKS_PER_TILE * q + n)
                    if n == 0:
                        sum_cross(i, q - 1)
                    if n == 1:
                        sum_pairs(i, q - 1)
                    if n in MLP_AFTER:
                        if isinstance(i, int) and MLP_AFTER[n] == 0:
                            pe.wait_ge(ring_emptied, JOBS)
                            pe.wait_ge(dense_w_loaded, 16 * STACK)
                        mlp_result(i, q - 1, MLP_AFTER[n])
                sum_triples(i, q)
                mlp_result(i, q - 1, RESULTS - 1)

            pe.wait_ge(small_copied, SMALL_BLOCKS)
            for n in range(BANKS_PER_TILE):
                triple_banks(0, n)
            weights_by_feature()
            sum_triples(0, 0)
            dense_by_feature()
            tile(0, 1)
            with pe.Fori(1, BLOCKS) as i:
                for q in range(TILES_PER_BLOCK):
                    tile(i, q)
            sum_cross_unfolded()
            sum_pairs(BLOCKS, -1)
            for r in range(RESULTS):
                mlp_result(BLOCKS, -1, r)

        @block.scalar
        def _(act):
            def filled(n):
                act.wait_ge(ring_filled, n + 1)
                return ring[n % len(ring)]

            for n, job in enumerate(ids_jobs):
                bank = filled(n)
                nc.scalar.copy(ids_wide[:, job[0]:job[-1] + 1, :],
                               bank[0:SMALL_PARTS, 0:NSMALL * P * len(job)].rearrange("p (t n) -> p t n", n=NSMALL * P)
                               ).then_inc(ring_emptied, 1)
            for n, job in enumerate(w2_jobs):
                bank = filled(W2_FROM + n)
                nc.scalar.copy(w2_t[:, job[0]:job[-1] + 1, :],
                               bank[:, 0:P * len(job)].rearrange("p (j h) -> p j h", h=P)).then_inc(ring_emptied, 1)
            for j in range(FIELDS):
                bank = filled(SUMS_FROM + j)
                nc.scalar.copy(sums[:, j, :], bank[:, 0:W]).then_inc(ring_emptied, 1)

            def weights_by_feature():
                for n, job in enumerate(wide1_jobs):
                    bank = filled(WIDE1_FROM + n)
                    nc.scalar.copy(weights1[0:FIRST, job[0]:job[-1] + 1, :],
                                   bank[0:FIRST, 0:P * len(job)].rearrange("p (j h) -> p j h", h=P)
                                   ).then_inc(ring_emptied, 1)
                for n, job in enumerate(wide2_jobs):
                    bank = filled(WIDE2_FROM + n)
                    nc.scalar.copy(weights2[0:GRAM, job[0]:job[-1] + 1, :],
                                   bank[0:GRAM, 0:P * len(job)].rearrange("p (j h) -> p j h", h=P)
                                   ).then_inc(ring_emptied, 1)
                act.wait_ge(small_loaded, 16 * SMALL_LOADS)

            def dense_by_feature():
                for n in range(len(dense_jobs)):
                    act.wait_ge(ring_filled, DENSE_FROM + n + 1)
                    nc.scalar.copy(dense_t[:, 4 * P * n:4 * P * (n + 1)], acc_mlp[n % 2][:, :]).then_inc(ring_emptied, 1)

            def await_sums():
                act.wait_ge(small_done, SMALL_BLOCKS)
                act.wait_ge(ring_emptied, WIDE1_FROM)
                act.wait_ge(wide_step, 1)

            def own_weights(d):
                for l0, n, row, wid in ((A0, NA, 0, FIELDS), (B0, NB_, ROW_B, WID_B), (C0, NC, ROW_C, NC)):
                    if d < n:
                        at = pair_column(l0, d)
                        for c0, num in ((l0, n), (ONE, 1)):
                            nc.scalar.copy(wide1[:, c0:c0 + num, at:at + n - d],
                                           pair_run(c0, num, row, wid, n, d)).then_inc(wide_own, 1)

            def copy_triples(i, n):
                q, first = divmod(n, BANKS_PER_TILE)
                if first == 0:
                    wait_for(act, z_done, through(i, q, 2, -2))
                act.wait_ge(triples_done, i * BANKS_PER_BLOCK + (n + 1))
                tokens = slice(BANK_STEPS * G * n, BANK_STEPS * G * (n + 1))
                nc.scalar.copy(
                    trip1[0:FIRST, :, tokens].rearrange("p j (t g) -> p t j g", g=G),
                    acc_first[n % 2][0:FIRST, 0:BANK_STEPS * FIELDS1 * G].rearrange(
                        "p (t j g) -> p t j g", j=FIELDS1, g=G)).then_inc(triples_copied, 1)
                nc.scalar.copy(
                    trip2[0:SECOND, :, tokens].rearrange("p j (t g) -> p t j g", g=G),
                    acc_second[n % 2][0:SECOND, 0:BANK_STEPS * SECOND_FIELDS * G].rearrange(
                        "p (t j g) -> p t j g", j=SECOND_FIELDS, g=G)[:, :, SECOND_FIELDS - KEPT:SECOND_FIELDS, :]
                ).then_inc(triples_copied, 1)

            def copy_second_sum(i, q):
                cols = columns(q)
                act.wait_ge(z_done, through(i, q, 2, 1))
                nc.scalar.activation(z[:, 1, cols], acc_z[1][:, cols], ACT.Identity,
                                     bias=bias[:, 0:1]).then_inc(z_copied, 1)

            def copy_first_sum(i, q):
                cols = columns(q)
                act.wait_ge(z_done, through(i, q, 2, 2))
                nc.scalar.copy(z[:, 0, cols], acc_z[0][:, cols]).then_inc(z_copied, 1)

            def copy_result(i, q, r):
                cols = columns(q)
                act.wait_ge(mlp_done, through(i, q, RESULTS, r + 1))
                if r < RES1:
                    ins = nc.scalar.activation(hid1[:, r, cols], acc_mlp[r % 2][:, cols], ACT.Relu,
                                               bias=bias_top1[:, r:r + 1])
                elif r < RES1 + RES2:
                    m = r - RES1
                    ins = nc.scalar.activation(hid2[:, m, cols], acc_mlp[r % 2][:, cols], ACT.Relu,
                                               bias=bias_top2[:, m:m + 1])
                else:
                    wait_for(act, y_stored, through(i, q, 16))
                    ins = nc.scalar.copy(y_now[:, cols], acc_mlp[r % 2][0:1, cols])
                ins.then_inc(mlp_copied, 1)

            def tile(i, q):
                for n in range(BANKS_PER_TILE):
                    copy_triples(i, BANKS_PER_TILE * q + n)
                    if n == 0:
                        copy_second_sum(i, q - 1)
                    if n == 1:
                        copy_first_sum(i, q - 1)
                    if n in MLP_AFTER:
                        copy_result(i, q - 1, MLP_AFTER[n])
                copy_result(i, q - 1, RESULTS - 1)

            act.wait_ge(dense_w_loaded, 16 * STACK)
            await_sums()
            own_weights(0)
            for n in range(BANKS_PER_TILE):
                copy_triples(0, n)
                own_weights(n + 1)
            weights_by_feature()
            dense_by_feature()
            tile(0, 1)
            with act.Fori(1, BLOCKS) as i:
                for q in range(TILES_PER_BLOCK):
                    tile(i, q)
            copy_second_sum(BLOCKS, -1)
            copy_first_sum(BLOCKS, -1)
            for r in range(RESULTS):
                copy_result(BLOCKS, -1, r)


_INS = (["dense_ctx", "ids"] + [f"tbl_{f}" for f in range(FIELDS)]
        + ["W_top1", "b_top1", "W_top2", "b_top2", "W_top3", "L0_rec_W1", "L0_rec_b1", "L0_rec_W2", "L0_rec_b2"])


def kernel(**inputs):
    import numpy as _np
    import concourse.bacc as _bacc
    from concourse import mybir as _mybir
    from concourse.bass_utils import run_bass_kernel_spmd as _run

    nc = _bacc.Bacc("TRN2", target_bir_lowering=False, num_devices=1)
    arrays, args = {}, []
    for name in _INS:
        a = _np.ascontiguousarray(inputs[name])
        arrays[f"in_{name}"] = a
        args.append(nc.dram_tensor(f"in_{name}", a.shape, _mybir.dt.from_np(a.dtype), kind="ExternalInput").ap())
    y = nc.dram_tensor("out_y", (TOKENS, 1), _mybir.dt.float32, kind="ExternalOutput").ap()
    build(nc, args[0], args[1], args[2:2 + FIELDS], *args[2 + FIELDS:], y)
    r = _run(nc, [arrays], core_ids=[0])
    return r.results[0]["out_y"]
```
